# Optimizing a Trainium2 kernel written in Bass

```python
import numpy as np
import jax
import jax.numpy as jnp

def _softmax(x, axis=-1):
    return jax.nn.softmax(x, axis=axis)

def _gelu(x):
    return jax.nn.gelu(x, approximate=True)

def _silu(x):
    return jax.nn.silu(x)

def _sigmoid(x):
    return jax.nn.sigmoid(x)

def _layernorm(x, axis=-1, eps=1e-05):
    m = jnp.mean(x, axis=axis, keepdims=True)
    v = jnp.var(x, axis=axis, keepdims=True)
    return (x - m) / jnp.sqrt(v + eps)

def _scatter_add(tgt, idx, src, axis=0):
    return tgt.at[idx].add(src)

def _segment_sum(src, seg, n):
    return jax.ops.segment_sum(src, seg, n)
kernel_name = 'mk_recurrent_d1_jaxref_r4_1e742a'

def setup_inputs(seed: int=0):
    np.random.seed(seed)
    _w = jnp.asarray

    def _L0_attn_setup():
        import jax, jax.numpy as jnp
        import numpy as np
        H = 16
        E = 256
        D = E // H
        M = 256
        EPS = 1e-12
        key = jax.random.key(seed)
        ks = jax.random.split(key, 12)
        s = 0.02
        B, S = (8, 256)
        return {'hidden_states': jax.random.normal(ks[0], (B, S, E), jnp.float32), 'Wq': jax.random.normal(ks[1], (E, E), jnp.float32) * s, 'bq': jnp.zeros((E,), jnp.float32), 'Wk': jax.random.normal(ks[2], (E, E), jnp.float32) * s, 'bk': jnp.zeros((E,), jnp.float32), 'Wv': jax.random.normal(ks[3], (E, E), jnp.float32) * s, 'bv': jnp.zeros((E,), jnp.float32), 'dist_emb': jax.random.normal(ks[4], (2 * M - 1, D), jnp.float32) * s, 'Wo': jax.random.normal(ks[5], (E, E), jnp.float32) * s, 'bo': jnp.zeros((E,), jnp.float32), 'ln_gamma': jnp.ones((E,), jnp.float32), 'ln_beta': jnp.zeros((E,), jnp.float32)}
    _L0_attn_in = _L0_attn_setup()

    def _L0_ffn_setup():
        import jax, jax.numpy as jnp
        import numpy as np
        TOP_K = 2
        EPS = 1e-05

        def layer_norm(x, g, b):
            mu = jnp.mean(x, axis=-1, keepdims=True)
            var = jnp.mean(jnp.square(x - mu), axis=-1, keepdims=True)
            return (x - mu) * jax.lax.rsqrt(var + EPS) * g + b
        key = jax.random.key(seed)
        ks = jax.random.split(key, 12)
        B, S, D, F, E = (2, 512, 256, 1024, 8)
        std = 0.02
        return {'x': jax.random.normal(ks[0], (B, S, D), jnp.float32), 'g1': jnp.ones((D,), jnp.float32), 'be1': jnp.zeros((D,), jnp.float32), 'mix_w': jax.random.normal(ks[1], (D, D), jnp.float32) * std, 'mix_b': jnp.zeros((D,), jnp.float32), 'g2': jnp.ones((D,), jnp.float32), 'be2': jnp.zeros((D,), jnp.float32), 'router_w': jax.random.normal(ks[2], (D, E), jnp.float32) * std, 'w1': jax.random.normal(ks[3], (E, D, F), jnp.float32) * std, 'b1': jnp.zeros((E, F), jnp.float32), 'w2': jax.random.normal(ks[4], (E, F, D), jnp.float32) * std, 'b2': jnp.zeros((E, D), jnp.float32)}
    _L0_ffn_in = _L0_ffn_setup()
    _d = {'L0_attn_hidden_states': _L0_attn_in['hidden_states'], 'L0_attn_Wq': _L0_attn_in['Wq'], 'L0_attn_bq': _L0_attn_in['bq'], 'L0_attn_Wk': _L0_attn_in['Wk'], 'L0_attn_bk': _L0_attn_in['bk'], 'L0_attn_Wv': _L0_attn_in['Wv'], 'L0_attn_bv': _L0_attn_in['bv'], 'L0_attn_dist_emb': _L0_attn_in['dist_emb'], 'L0_attn_Wo': _L0_attn_in['Wo'], 'L0_attn_bo': _L0_attn_in['bo'], 'L0_attn_ln_gamma': _L0_attn_in['ln_gamma'], 'L0_attn_ln_beta': _L0_attn_in['ln_beta'], 'L0_ffn_g1': _L0_ffn_in['g1'], 'L0_ffn_be1': _L0_ffn_in['be1'], 'L0_ffn_mix_w': _L0_ffn_in['mix_w'], 'L0_ffn_mix_b': _L0_ffn_in['mix_b'], 'L0_ffn_g2': _L0_ffn_in['g2'], 'L0_ffn_be2': _L0_ffn_in['be2'], 'L0_ffn_router_w': _L0_ffn_in['router_w'], 'L0_ffn_w1': _L0_ffn_in['w1'], 'L0_ffn_b1': _L0_ffn_in['b1'], 'L0_ffn_w2': _L0_ffn_in['w2'], 'L0_ffn_b2': _L0_ffn_in['b2']}
    _x0 = _d['L0_attn_hidden_states']
    _d['L0_attn_hidden_states'] = jax.random.normal(jax.random.fold_in(jax.random.key(seed), 1), (8, 512, 256), dtype=_x0.dtype)
    del _x0
    return _d

def reference(L0_attn_hidden_states, L0_attn_Wq, L0_attn_bq, L0_attn_Wk, L0_attn_bk, L0_attn_Wv, L0_attn_bv, L0_attn_dist_emb, L0_attn_Wo, L0_attn_bo, L0_attn_ln_gamma, L0_attn_ln_beta, L0_ffn_g1, L0_ffn_be1, L0_ffn_mix_w, L0_ffn_mix_b, L0_ffn_g2, L0_ffn_be2, L0_ffn_router_w, L0_ffn_w1, L0_ffn_b1, L0_ffn_w2, L0_ffn_b2):

    def _L0_attn_ref(hidden_states, Wq, bq, Wk, bk, Wv, bv, dist_emb, Wo, bo, ln_gamma, ln_beta):
        import jax, jax.numpy as jnp
        import numpy as np
        H = 16
        E = 256
        D = E // H
        M = 256
        EPS = 1e-12
        B, S, _ = hidden_states.shape

        def heads(x):
            return x.reshape(B, S, H, D).transpose(0, 2, 1, 3)
        q = heads(hidden_states @ Wq + bq)
        k = heads(hidden_states @ Wk + bk)
        v = heads(hidden_states @ Wv + bv)
        scores = jnp.einsum('bhqd,bhkd->bhqk', q, k)
        pos_l = jnp.arange(S)[:, None]
        pos_r = jnp.arange(S)[None, :]
        dist_idx = pos_l - pos_r + M - 1
        pos_emb = dist_emb[dist_idx]
        rel_q = jnp.einsum('bhld,lrd->bhlr', q, pos_emb)
        rel_k = jnp.einsum('bhrd,lrd->bhlr', k, pos_emb)
        scores = (scores + rel_q + rel_k) / jnp.sqrt(jnp.asarray(D, scores.dtype))
        probs = jax.nn.softmax(scores, axis=-1)
        ctx = jnp.einsum('bhqk,bhkd->bhqd', probs, v)
        ctx = ctx.transpose(0, 2, 1, 3).reshape(B, S, E)
        h = ctx @ Wo + bo + hidden_states
        mu = jnp.mean(h, axis=-1, keepdims=True)
        var = jnp.mean(jnp.square(h - mu), axis=-1, keepdims=True)
        out = (h - mu) * jax.lax.rsqrt(var + EPS) * ln_gamma + ln_beta
        return out

    def _L0_ffn_ref(x, g1, be1, mix_w, mix_b, g2, be2, router_w, w1, b1, w2, b2):
        import jax, jax.numpy as jnp
        import numpy as np
        TOP_K = 2
        EPS = 1e-05

        def layer_norm(x, g, b):
            mu = jnp.mean(x, axis=-1, keepdims=True)
            var = jnp.mean(jnp.square(x - mu), axis=-1, keepdims=True)
            return (x - mu) * jax.lax.rsqrt(var + EPS) * g + b
        res = x
        n = layer_norm(x, g1, be1)
        x = res + n + (n @ mix_w + mix_b)
        res = x
        n = layer_norm(x, g2, be2)
        B, S, D = n.shape
        E = w1.shape[0]
        flat = n.reshape(-1, D)
        probs = jax.nn.softmax(flat @ router_w, axis=-1)
        topw, topi = jax.lax.top_k(probs, TOP_K)
        combine = jnp.sum(jax.nn.one_hot(topi, E, dtype=flat.dtype) * topw[..., None], axis=1)
        h = jax.nn.silu(jnp.einsum('td,edf->tef', flat, w1) + b1)
        y = jnp.einsum('tef,efd->ted', h, w2) + b2
        out = jnp.einsum('te,ted->td', combine, y)
        return res + out.reshape(B, S, D)
    x = L0_attn_hidden_states
    xn = _layernorm(x, axis=-1)
    s = _L0_attn_ref(xn, L0_attn_Wq, L0_attn_bq, L0_attn_Wk, L0_attn_bk, L0_attn_Wv, L0_attn_bv, L0_attn_dist_emb, L0_attn_Wo, L0_attn_bo, L0_attn_ln_gamma, L0_attn_ln_beta)
    g = _silu(_L0_ffn_ref(xn, L0_ffn_g1, L0_ffn_be1, L0_ffn_mix_w, L0_ffn_mix_b, L0_ffn_g2, L0_ffn_be2, L0_ffn_router_w, L0_ffn_w1, L0_ffn_b1, L0_ffn_w2, L0_ffn_b2))
    x = x + s * g
    return x

_drawn_inputs = setup_inputs


def setup_inputs(seed=0):
    import zlib

    import numpy as np

    out = dict(_drawn_inputs(seed))
    spreads = {'L0_attn_bq': (0.0, 0.8),
     'L0_attn_bk': (0.0, 0.8),
     'L0_attn_bv': (0.0, 0.565),
     'L0_attn_bo': (0.0, 0.1),
     'L0_attn_ln_gamma': (1.0, 0.2),
     'L0_attn_ln_beta': (0.0, 0.1),
     'L0_ffn_g1': (1.0, 0.2),
     'L0_ffn_be1': (0.0, 0.278),
     'L0_ffn_mix_b': (0.0, 0.328),
     'L0_ffn_g2': (1.0, 0.6),
     'L0_ffn_be2': (0.0, 0.8),
     'L0_ffn_b1': (0.0, 0.8),
     'L0_ffn_b2': (0.0, 0.8)}
    factors = {'L0_attn_Wq': 8.0,
     'L0_attn_Wk': 8.0,
     'L0_attn_Wv': 8.0,
     'L0_attn_dist_emb': 8.0,
     'L0_attn_Wo': 4.132,
     'L0_ffn_router_w': 6.881,
     'L0_ffn_w1': 8.0,
     'L0_ffn_w2': 7.85}
    for name, (base, spread) in spreads.items():
        noise = np.random.default_rng([zlib.crc32(name.encode()), seed]).standard_normal(out[name].shape)
        drawn = base * np.exp(spread * noise) if base else spread * noise
        out[name] = jnp.asarray(drawn.astype(out[name].dtype))
    for name, factor in factors.items():
        out[name] = (out[name] * factor).astype(out[name].dtype)
    return out
```

```python
from contextlib import ExitStack

import concourse.bass as bass
from concourse import mybir

F32 = mybir.dt.float32
BF16 = mybir.dt.bfloat16
I32 = mybir.dt.int32
ALU = mybir.AluOpType
ACT = mybir.ActivationFunctionType
AX = mybir.AxisListType

P = 128
B, S, E = 8, 512, 256
H, D = 16, 16
M_POS = 256
NE, F = 8, 1024
TOPK = 2
BH = B * H
ST = S // P
NT = B * ST
KC = E // P
FC = F // P
DA = D + 1
PARTS = 3
PAIRS = [(0, 0), (0, 1), (1, 0), (1, 1), (0, 2), (2, 0)]
KS = D * len(PAIRS)
WIN = 2 * S
LB = 64
RU = 16
PITCH = S * S + 1024
ONE = 1
EPS_LN, EPS_ATT = 1e-5, 1e-12
SM_SCALE = float(D) ** -0.5
VECS = ["bv", "bo", "mix_b", "g1", "be1", "g2", "be2", "ln_gamma", "ln_beta"]


def start_at_one(nc, sems, free=()):
    with nc.Block() as block:
        @block.gpsimd
        def _(pool):
            for s in sems:
                pool.sem_inc(s, ONE)
            for s, n in free:
                pool.sem_inc(s, n)


def wait(eng, sem, value):
    if isinstance(value, int) and value <= 0:
        return
    eng.wait_ge(sem, value + ONE)


class Steps:

    def __init__(self, eng, sem, base, spare=None):
        self.eng, self.sem, self.base, self.n, self.spare = eng, sem, base, 0, spare

    def did(self, ins):
        ins.then_inc(self.sem, 1)
        self.n += 1

    def settle(self):
        wait(self.eng, self.sem, self.base + self.n)

    def settle_apart(self):
        self.settle()
        self.eng.memset(self.spare, 0.0)


def paired(eng, n, first, second):
    first(0, 0)
    with eng.Fori(0, (n - 2) // 2) as i:
        first(i * 2 + 1, 1)
        second(i * 2, 0)
        first(i * 2 + 2, 0)
        second(i * 2 + 1, 1)
    first(n - 1, 1)
    second(n - 2, 0)
    second(n - 1, 1)


def over_tiles(vec, n):
    return vec.unsqueeze(1).to_broadcast([P, n, E])


def inverse_sqrt(nc, step, var, eps, work):
    ve, a, y = (work[:, i] for i in range(3))
    step.did(nc.vector.tensor_scalar(ve, var, eps, None, ALU.add))
    step.settle()
    step.did(nc.vector.tensor_scalar(a.bitcast(I32), ve.bitcast(I32), 1, None, ALU.logical_shift_right))
    step.settle()
    step.did(nc.vector.tensor_scalar(y.bitcast(I32), a.bitcast(I32), -1, 0x5F3759DF, ALU.mult, ALU.add))
    step.settle()
    for _ in range(3):
        step.did(nc.vector.tensor_tensor(a, y, y, ALU.mult))
        step.settle()
        step.did(nc.vector.tensor_tensor(a, a, ve, ALU.mult))
        step.settle()
        step.did(nc.vector.tensor_scalar(a, a, -0.5, 1.5, ALU.mult, ALU.add))
        step.settle()
        step.did(nc.vector.tensor_tensor(y, y, a, ALU.mult))
        step.settle()


NORM_STEPS = 3 * ST + 15


def normalize(nc, step, src, dst, eps, stats):
    st, mv, work = stats
    for i in range(ST):
        step.did(nc.vector.bn_stats(st[:, i], src[:, i]))
    step.settle_apart()
    for i in range(ST):
        step.did(nc.vector.bn_aggr(mv[:, i], st[:, i]))
    step.settle()
    inverse_sqrt(nc, step, mv[:, :, 1], eps, work)
    for i in range(ST):
        step.did(nc.vector.tensor_scalar(dst[:, i], src[:, i], mv[:, i, 0:1], work[:, 2, i:i + 1], ALU.subtract, ALU.mult))
    step.settle()


def prep(nc, t, keep):
    with ExitStack() as ctx:
        def sb(name, shape, dt=F32):
            return ctx.enter_context(nc.sbuf_tensor(name, shape, dt))

        sems = []

        def sem(name):
            sems.append(ctx.enter_context(nc.semaphore(name)))
            return sems[-1]

        def dma_sem(name):
            return ctx.enter_context(nc.semaphore(name))

        ident = keep["ident"]
        acc, comb, tabq, tabk = keep["acc"], keep["comb"], keep["tabq"], keep["tabk"]
        bank = [ctx.enter_context(nc.psum_tensor(f"prep_bank{i}", [P, 512], F32)) for i in range(8)]
        vec = sb("vecs", [P, len(VECS), E])
        V = {n: vec[:, i, :] for i, n in enumerate(VECS)}
        wq, wk, wv, mix = (sb(n, [P, KC, E]) for n in ("wq_sb", "wk_sb", "wv_sb", "mix_sb"))
        rw = sb("router_sb", [P, KC, NE])
        b2 = sb("b2_sb", [NE, E])
        bqk = sb("bqk_sb", [P, 4])
        mask = sb("mask_sb", [KS, 2])
        tab32 = sb("tab32", [KS, 2, WIN])
        tmp32 = sb("tmp32", [KS, WIN])
        tabh = sb("tabh", [KS, WIN], BF16)
        xs = sb("xs", [P, 2, ST, E])
        xn = sb("xn", [P, 2, ST, E])
        n1 = sb("n1", [P, 2, ST, E])
        n1r = sb("n1r", [P, ST, E])
        xb = sb("xn_plus_bo", [P, ST, E])
        xm = sb("xn_plus_mixb", [P, 2, ST, E])
        stats1, stats2 = ((sb(f"bn_stats{i}", [P, ST, 6]), sb(f"bn_mv{i}", [P, ST, 2]), sb(f"bn_work{i}", [P, 3, ST]))
                          for i in range(2))
        xnT = sb("xnT", [P, 2, KC, S])
        n1T = sb("n1T", [P, 2, KC, S])
        qk32 = sb("qk32", [P, 4, S])
        qkr = sb("qkr", [P, 4, S])
        part = [sb(f"part{i}", [P, 4, S], BF16) for i in range(PARTS)]
        va = sb("va", [P, ST, H, DA])
        zero = sb("zero", [P, 1])
        s_zero = sem("zero_set")
        n2 = sb("n2", [P, ST, E])
        n2T = sb("n2T", [P, KC, S])
        pr = sb("probs8", [P, ST, NE])
        rest = sb("rest8", [P, ST, NE])
        top = sb("top8", [P, ST, 8])
        m8 = sb("m8", [P, ST, 1])
        cb = sb("cb", [P, ST, NE])
        cT = sb("cT", [NE, S])

        s_const, s_xb_st, s_va_st, s_n2_st, s_part_st = (sem(n) for n in (
            "const_loaded", "xb_stored", "va_stored", "n2T_stored", "parts_stored"))
        s_x = [sem(f"x_loaded{i}") for i in range(2)]
        s_one, s_tab = sem("ones_set"), sem("tab_steps")
        s_d1, s_d2, s_d3 = sem("dve_first"), sem("dve_second"), sem("dve_router")
        s_xn, s_n1 = sem("xn_ready"), sem("n1_ready")
        s_pool = sem("pool_steps")
        s_tx, s_tn, s_qkp, s_vmp = sem("xn_turned"), sem("n1_turned"), sem("qk_product"), sem("vmix_product")
        s_cx, s_cn, s_qk = sem("xnT_copied"), sem("n1T_copied"), sem("qk_copied")
        s_vu, s_mu = sem("v_taken"), sem("mix_taken")
        s_n2, s_t2, s_c2, s_lg = sem("n2_ready"), sem("n2_turned"), sem("n2T_copied"), sem("logits_ready")
        s_sh, s_ex, s_cb = sem("logits_shifted"), sem("exp8_done"), sem("comb_ready")
        s_ct, s_cc, s_b2p, s_b2u = sem("comb_turned"), sem("combT_copied"), sem("b2_product"), sem("b2_added")
        NCONST = 12
        POOL_N = 6
        spare = sb("spare", [P, 1])

        start_at_one(nc, sems)
        block = ctx.enter_context(nc.Block())

        @block.sync
        def _(sp):
            sp.dma_start(ident[:], t["ident"]).then_inc(s_const, 16)
            for dst, src in ((wq, "Wq"), (wk, "Wk"), (wv, "Wv"), (mix, "mix_w"), (rw, "router_w")):
                sp.dma_start(dst[:], t[src].rearrange("(k p) n -> p k n", p=P)).then_inc(s_const, 16)
            sp.dma_start(vec[:], t["vecs"].partition_broadcast(P)).then_inc(s_const, 16)
            sp.dma_start(b2[:], t["b2"]).then_inc(s_const, 16)
            sp.dma_start(bqk[:], t["bqk"]).then_inc(s_const, 16)
            sp.dma_start(mask[:], t["mask"]).then_inc(s_const, 16)
            for i, name in enumerate(("tabq", "tabk")):
                sp.dma_start(tab32[:, i], t[name]).then_inc(s_const, 16)

            def load(g, par):
                wait(sp, s_xn, g - 1)
                sp.dma_start(xs[:, par], t["x"][bass.ds(g * S, S)].rearrange("(t p) e -> p t e", p=P)).then_inc(s_x[par], 16)

            def store(g, par):
                sp.wait_ge(s_pool, g * POOL_N + 1 + ONE)
                sp.dma_start(t["xnbo"][bass.ds(g * S, S)].rearrange("(t p) e -> p t e", p=P), xb[:]).then_inc(s_xb_st, 16)
                sp.wait_ge(s_pool, g * POOL_N + POOL_N + ONE)
                for i in range(PARTS):
                    for c in range(4):
                        dst = (t["qparts"], t["kparts"])[c // 2]
                        dst = dst[i, bass.ds(g, 1)].rearrange("o (c p) s -> (o c) p s", c=2)[c % 2]
                        sp.dma_start(dst, part[i][:, c]).then_inc(s_part_st, 16)
                sp.wait_ge(s_vu, (g + 1) * ST + ONE)
                sp.dma_start(t["va"][bass.ds(g * S, S)].rearrange("(t p) h d -> p t (h d)", p=P),
                             va[:].rearrange("p t h d -> p t (h d)")).then_inc(s_va_st, 16)

            def second(g, par):
                dst = t["flatT"][bass.ds(g * P, P)]
                sp.wait_ge(s_c2, (g + 1) * KC + ONE)
                sp.dma_start(dst, n2T[:]).then_inc(s_n2_st, 16)

            def first(g, par):
                if not (isinstance(g, int) and g == B - 1):
                    load(g + 1, 1 - par)
                store(g, par)

            load(0, 0)

            paired(sp, B, first, second)
            sp.wait_ge(s_xb_st, 16 * B + ONE)
            sp.wait_ge(s_part_st, 16 * B * PARTS * 4 + ONE)
            sp.wait_ge(s_va_st, 16 * B + ONE)
            sp.wait_ge(s_n2_st, 16 * B + ONE)

        @block.gpsimd
        def _(pool):
            nc.gpsimd.memset(va[:], 1.0).then_inc(s_one, 1)
            nc.gpsimd.memset(zero[:], 0.0).then_inc(s_zero, 1)
            pool.wait_ge(s_zero, 1 + ONE)
            zeros = zero[:].unsqueeze(2).to_broadcast([P, 4, S])
            pool.wait_ge(s_const, 16 * NCONST + ONE)

            def first(g, par):
                step = Steps(pool, s_pool, g * POOL_N)
                pool.wait_ge(s_xn, g + 1 + ONE)
                wait(pool, s_xb_st, 16 * g)
                step.did(nc.gpsimd.tensor_tensor(xb[:], xn[:, par], over_tiles(V["bo"], ST), ALU.add))
                wait(pool, s_n2, g - 1)
                step.did(nc.gpsimd.tensor_tensor(xm[:, par], xn[:, par], over_tiles(V["mix_b"], ST), ALU.add))
                pool.wait_ge(s_qk, 4 * (g + 1) + ONE)
                wait(pool, s_part_st, 16 * PARTS * 4 * g)
                step.did(nc.gpsimd.tensor_tensor(part[0][:], qk32[:], zeros, ALU.add))
                step.settle()
                step.did(nc.gpsimd.tensor_tensor(qkr[:], qk32[:], part[0][:], ALU.subtract))
                step.settle()
                step.did(nc.gpsimd.tensor_tensor(part[1][:], qkr[:], zeros, ALU.add))
                step.settle()
                step.did(nc.gpsimd.tensor_tensor(part[2][:], qkr[:], part[1][:], ALU.subtract))

            paired(pool, B, first, lambda g, par: None)

        @block.scalar
        def _(act):
            act.wait_ge(s_const, 16 * NCONST + ONE)

            def first(g, par):
                for k in range(KC):
                    act.wait_ge(s_tx, (g * KC) + k + 1 + ONE)
                    nc.scalar.copy(xnT[:, par, k], bank[k][:]).then_inc(s_cx, 1)
                for k in range(KC):
                    act.wait_ge(s_tn, (g * KC) + k + 1 + ONE)
                    nc.scalar.copy(n1T[:, par, k], bank[2 + k][:]).then_inc(s_cn, 1)
                wait(act, s_pool, g * POOL_N)
                for c in range(4):
                    act.wait_ge(s_qkp, g * 4 + c + 1 + ONE)
                    nc.scalar.activation(qk32[:, c], bank[4 + c % 2][:], ACT.Identity, bias=bqk[:, c:c + 1]).then_inc(s_qk, 1)

            def second(g, par):
                wait(act, s_n2_st, 16 * g)
                for k in range(KC):
                    act.wait_ge(s_t2, g * KC + k + 1 + ONE)
                    nc.scalar.copy(n2T[:, k], bank[k][:]).then_inc(s_c2, 1)
                act.wait_ge(s_sh, g + 1 + ONE)
                nc.scalar.activation(pr[:], pr[:], ACT.Exp).then_inc(s_ex, 1)
                act.wait_ge(s_ct, g + 1 + ONE)
                nc.scalar.copy(cT[:], bank[3][0:NE, :]).then_inc(s_cc, 1)

            paired(act, B, first, second)

        @block.vector
        def _(dve):
            dve.wait_ge(s_const, 16 * NCONST + ONE)
            tab = Steps(dve, s_tab, 0)

            def split_table(dst, i):
                tab.did(nc.vector.tensor_copy(tabh[:], tab32[:, i]))
                tab.settle()
                tab.did(nc.vector.scalar_tensor_tensor(tmp32[:], tabh[:], mask[:, 0:1], tab32[:, i], ALU.mult, ALU.add))
                tab.settle()
                tab.did(nc.vector.tensor_copy(tabh[:], tmp32[:]))
                tab.settle()
                tab.did(nc.vector.scalar_tensor_tensor(dst[:], tabh[:], mask[:, 1:2], tmp32[:], ALU.mult, ALU.add))

            split_table(tabq, 0)
            tab.settle()
            split_table(tabk, 1)
            tab.settle()
            D1 = 2 * NORM_STEPS + 2

            def norm(step, src, dst, stats):
                normalize(nc, step, src, dst, EPS_LN, stats)

            def first(g, par):
                step = Steps(dve, s_d1, g * D1, spare[:])
                dve.wait_ge(s_x[par], (g + 2 - par) * 8 + ONE)
                wait(dve, s_pool, (g - 1) * POOL_N)
                wait(dve, s_tx, (g - 1) * KC)
                norm(step, xs[:, par], xn[:, par], stats1)
                nc.vector.memset(spare[:], 0.0).then_inc(s_xn, 1)
                norm(step, xn[:, par], n1r, stats1)
                wait(dve, s_tn, (g - 1) * KC)
                step.did(nc.vector.tensor_tensor(n1r[:], n1r[:], over_tiles(V["g1"], ST), ALU.mult))
                step.settle()
                step.did(nc.vector.tensor_tensor(n1[:, par], n1r[:], over_tiles(V["be1"], ST), ALU.add))
                step.settle()
                nc.vector.memset(spare[:], 0.0).then_inc(s_n1, 1)
                wait(dve, s_va_st, 16 * g)
                dve.wait_ge(s_one, 1 + ONE)
                dve.wait_ge(s_pool, g * POOL_N + 2 + ONE)
                for i in range(ST):
                    dve.wait_ge(s_vmp, g * ST + i + 1 + ONE)
                    pv = bank[6 + i % 2]
                    nc.vector.tensor_tensor(va[:, i, :, 0:D], pv[:, 0:E].rearrange("p (h d) -> p h d", h=H),
                                            V["bv"].rearrange("p (h d) -> p h d", h=H), ALU.add).then_inc(s_vu, 1)
                    nc.vector.tensor_tensor(n1[:, par, i], n1[:, par, i], pv[:, E:2 * E], ALU.add).then_inc(s_mu, 1)

            D2 = 2 + NORM_STEPS + 2
            D3 = 7 + 2 * ST

            def second(g, par):
                step = Steps(dve, s_d2, g * D2, spare[:])
                dve.wait_ge(s_mu, (g + 1) * ST + ONE)
                dve.wait_ge(s_pool, g * POOL_N + 2 + ONE)
                x1 = acc[:, bass.ds(g * ST, ST)]
                wait(dve, s_t2, g * KC)
                step.did(nc.vector.tensor_tensor(n2[:], n1[:, par], xm[:, par], ALU.add))
                step.settle()
                step.did(nc.vector.tensor_copy(x1, n2[:]))
                norm(step, n2, n1[:, par], stats2)
                step.did(nc.vector.tensor_tensor(n1[:, par], n1[:, par], over_tiles(V["g2"], ST), ALU.mult))
                step.settle()
                step.did(nc.vector.tensor_tensor(n2[:], n1[:, par], over_tiles(V["be2"], ST), ALU.add))
                step.settle()
                nc.vector.memset(spare[:], 0.0).then_inc(s_n2, 1)
                r = Steps(dve, s_d3, g * D3, spare[:])
                dve.wait_ge(s_lg, g + 1 + ONE)
                lg = bank[2][:, 0:ST * NE].rearrange("p (t e) -> p t e", t=ST)
                r.did(nc.vector.tensor_reduce(m8[:], lg, AX.X, ALU.max))
                r.settle()
                nc.vector.tensor_tensor(pr[:], lg, m8[:].to_broadcast([P, ST, NE]), ALU.subtract).then_inc(s_sh, 1)
                dve.wait_ge(s_ex, g + 1 + ONE)
                r.did(nc.vector.tensor_reduce(m8[:], pr[:], AX.X, ALU.add))
                r.settle()
                r.did(nc.vector.reciprocal(m8[:], m8[:]))
                r.settle()
                r.did(nc.vector.tensor_tensor(pr[:], pr[:], m8[:].to_broadcast([P, ST, NE]), ALU.mult))
                r.settle_apart()
                for i in range(ST):
                    r.did(nc.vector.max(top[:, i], pr[:, i]))
                r.settle()
                r.did(nc.vector.memset(top[:, :, TOPK:8], -1.0))
                r.settle_apart()
                for i in range(ST):
                    r.did(nc.vector.match_replace(rest[:, i], top[:, i], pr[:, i], 0.0))
                r.settle()
                r.did(nc.vector.tensor_tensor(cb[:], pr[:], rest[:], ALU.subtract))
                r.settle()
                r.did(nc.vector.tensor_copy(comb[:, bass.ds(g * ST, ST)], cb[:]))
                r.settle()
                nc.vector.memset(spare[:], 0.0).then_inc(s_cb, 1)
                dve.wait_ge(s_b2p, g + 1 + ONE)
                for i in range(2):
                    a2 = acc[:, bass.ds(g * ST + i * 2, 2)]
                    nc.vector.tensor_tensor(a2, a2, bank[4 + i][:].rearrange("p (t e) -> p t e", t=2),
                                            ALU.add).then_inc(s_b2u, 1)

            paired(dve, B, first, second)
            dve.wait_ge(s_b2u, 2 * B + ONE)

        @block.tensor
        def _(pe):
            pe.wait_ge(s_const, 16 * NCONST + ONE)

            def turn(dst, src, done):
                for k in range(KC):
                    for i in range(ST):
                        last = nc.tensor.transpose(dst[k][:, i * P:(i + 1) * P], src[:, i, k * P:(k + 1) * P], ident[:])
                    last.then_inc(done, 1)

            def first(g, par):
                pe.wait_ge(s_xn, g + 1 + ONE)
                turn(bank[0:2], xn[:, par], s_tx)
                pe.wait_ge(s_n1, g + 1 + ONE)
                turn(bank[2:4], n1[:, par], s_tn)
                pe.wait_ge(s_cx, KC * (g + 1) + ONE)
                wait(pe, s_b2u, 2 * (g - 1))
                for c in range(4):
                    if c >= 2:
                        pe.wait_ge(s_qk, g * 4 + c - 1 + ONE)
                    w = (wq, wk)[c // 2]
                    for k in range(KC):
                        last = nc.tensor.matmul(bank[4 + c % 2][:], w[:, k, (c % 2) * P:(c % 2 + 1) * P],
                                                xnT[:, par, k], start=(k == 0), stop=(k == KC - 1))
                    last.then_inc(s_qkp, 1)
                pe.wait_ge(s_cn, KC * (g + 1) + ONE)
                for i in range(ST):
                    wait(pe, s_mu, g * ST + i - 1)
                    for k in range(KC):
                        nc.tensor.matmul(bank[6 + i % 2][:, 0:E], xnT[:, par, k, i * P:(i + 1) * P], wv[:, k],
                                         start=(k == 0), stop=(k == KC - 1))
                    for k in range(KC):
                        last = nc.tensor.matmul(bank[6 + i % 2][:, E:2 * E], n1T[:, par, k, i * P:(i + 1) * P],
                                                mix[:, k], start=(k == 0), stop=(k == KC - 1))
                    last.then_inc(s_vmp, 1)

            def second(g, par):
                pe.wait_ge(s_n2, g + 1 + ONE)
                turn(bank[0:2], n2, s_t2)
                pe.wait_ge(s_c2, KC * (g + 1) + ONE)
                for i in range(ST):
                    for k in range(KC):
                        last = nc.tensor.matmul(bank[2][:, i * NE:(i + 1) * NE], n2T[:, k, i * P:(i + 1) * P],
                                                rw[:, k], start=(k == 0), stop=(k == KC - 1))
                last.then_inc(s_lg, 1)
                pe.wait_ge(s_cb, g + 1 + ONE)
                for i in range(ST):
                    last = nc.tensor.transpose(bank[3][0:NE, i * P:(i + 1) * P], cb[:, i], ident[:])
                last.then_inc(s_ct, 1)
                pe.wait_ge(s_cc, g + 1 + ONE)
                if isinstance(g, int) and g == B - 1:
                    pe.wait_ge(s_qk, 4 * B + ONE)
                else:
                    pe.wait_ge(s_qk, (g + 2) * 4 + ONE)
                for i in range(ST):
                    last = nc.tensor.matmul(bank[4 + i // 2][:, (i % 2) * E:(i % 2 + 1) * E], cT[:, i * P:(i + 1) * P],
                                            b2[:], start=True, stop=True)
                last.then_inc(s_b2p, 1)

            paired(pe, B, first, second)


def experts(nc, t, keep):
    with ExitStack() as ctx:
        def sb(name, shape, dt=F32):
            return ctx.enter_context(nc.sbuf_tensor(name, shape, dt))

        sems = []

        def sem(name):
            sems.append(ctx.enter_context(nc.semaphore(name)))
            return sems[-1]

        def dma_sem(name):
            return ctx.enter_context(nc.semaphore(name))

        acc, comb, tabq, tabk = keep["acc"], keep["comb"], keep["tabq"], keep["tabk"]
        up = [ctx.enter_context(nc.psum_tensor(f"up{i}", [P, 512], F32)) for i in range(2)]
        dn = [ctx.enter_context(nc.psum_tensor(f"dn{i}", [P, 512], F32)) for i in range(2)]
        rl = [ctx.enter_context(nc.psum_tensor(f"rl{i}", [P, 2, 512], F32)) for i in range(2)]
        w1 = [sb(f"w1_{i}", [P, KC, F]) for i in range(2)]
        w2 = [sb(f"w2_{i}", [P, FC, E]) for i in range(2)]
        b1 = sb("b1_sb", [P, NE, FC])
        tok = sb("tok", [P, B, KC, S])
        hid = sb("hid", [P, FC, S])
        stack = [sb(f"stack{i}", [KS, BH, LB], BF16) for i in range(2)]
        rel = sb("rel", [P, 4, 4, S])

        s_b1 = dma_sem("b1_loaded")
        s_w = [sem(f"w_loaded{i}") for i in range(2)]
        s_st = [sem(f"stack_loaded{i}") for i in range(2)]
        s_tok = dma_sem("tok_loaded")
        s_up, s_h, s_dn, s_y = sem("up_done"), sem("hid_ready"), sem("down_done"), sem("y_added")
        s_rm, s_ra, s_rv = sem("rel_done"), sem("rel_by_act"), sem("rel_by_dve")
        s_rs = [sem(f"rel_stored{i}") for i in range(4)]
        GH = B // 2

        start_at_one(nc, sems)
        block = ctx.enter_context(nc.Block())

        def steps(eng, body):
            with eng.Fori(0, NE // 2) as e2:
                for par in range(2):
                    for half in range(2):
                        with eng.Fori(0, GH) as gi:
                            body(e2 * 2 + par, e2, par, half, gi)

        def number(e, half, gi):
            return e * (2 * GH) + half * GH + gi

        @block.sync
        def _(sp):
            def body(e, e2, par, half, gi):
                n = number(e, half, gi)
                dst = (t["relq"], t["relk"])[half]
                for j in range(4):
                    sp.wait_ge(s_ra, n * 4 + j + 1 + ONE)
                    sp.wait_ge(s_rv, n * 4 + j + 1 + ONE)
                    at = (e * LB + gi * RU + j * 4) * S
                    sp.dma_start(dst[:, bass.ds(at, 4 * S)], rel[:, j].rearrange("p u s -> p (u s)")).then_inc(s_rs[j], 16)

            steps(sp, body)
            for j in range(4):
                sp.wait_ge(s_rs[j], 16 * NE * 2 * GH + ONE)

        @block.gpsimd
        def _(pool):
            pool.dma_start(b1[:], t["b1"]).then_inc(s_b1, 16)
            pool.dma_start(tok[:], t["flatT"].rearrange("(b p) k s -> p b k s", p=P)).then_inc(s_tok, 16)

        @block.scalar
        def _(act):
            def load_weights(e, par):
                wait(act, s_dn, (e - 1) * (2 * GH * ST))
                act.dma_start(w1[par][:], t["w1"][bass.ds(e, 1)].rearrange("o (k p) f -> p (o k) f", p=P)).then_inc(s_w[par], 16)
                act.dma_start(w2[par][:], t["w2"][bass.ds(e, 1)].rearrange("o (k p) d -> p (o k) d", p=P)).then_inc(s_w[par], 16)

            def load_stack(e, half):
                wait(act, s_rm, (e * 2 - 1 + half) * (GH * FC))
                for i, pair in enumerate(PAIRS):
                    src = (t["qparts"], t["kparts"])[half][pair[0]]
                    src = src.rearrange("b (h d) s -> d (b h) s", d=D)[:, :, bass.ds(e * LB, LB)]
                    act.dma_start(stack[half][i * D:(i + 1) * D], src).then_inc(s_st[half], 16)

            def turn(e, par, last=False):
                load_stack(e, 1)
                with act.Fori(0, GH) as gi:
                    body(e, None, par, 0, gi)
                if not last:
                    load_weights(e + 1, 1 - par)
                    load_stack(e + 1, 0)
                with act.Fori(0, GH) as gi:
                    body(e, None, par, 1, gi)

            def body(e, e2, par, half, gi):
                n = number(e, half, gi)
                for j in range(4):
                    for f in (2 * j, 2 * j + 1):
                        act.wait_ge(s_up, n * FC + f + 1 + ONE)
                        nc.scalar.activation(hid[:, f], up[f % 2][:], ACT.Silu,
                                             bias=b1[:, bass.ds(e, 1), f:f + 1].rearrange("p a b -> p (a b)")).then_inc(s_h, 1)
                    act.wait_ge(s_rm, n * FC + 2 * j + 1 + ONE)
                    act.wait_ge(s_rs[j], n * 16 + ONE)
                    nc.scalar.copy(rel[:, j, 0:2], rl[0][:]).then_inc(s_ra, 1)

            load_weights(0, 0)
            load_stack(0, 0)
            act.wait_ge(s_b1, 16)
            with act.Fori(0, NE // 2 - 1) as e2:
                for par in range(2):
                    turn(e2 * 2 + par, par)
            turn(NE - 2, 0)
            turn(NE - 1, 1, last=True)

        @block.vector
        def _(dve):
            def body(e, e2, par, half, gi):
                n = number(e, half, gi)
                g = gi + half * GH
                wait(dve, s_y, n * ST)
                for j in range(4):
                    dve.wait_ge(s_rm, n * 8 + 2 * j + 2 + ONE)
                    wait(dve, s_rs[j], n * 16)
                    nc.vector.tensor_copy(rel[:, j, 2:4], rl[1][:]).then_inc(s_rv, 1)
                for i in range(ST):
                    dve.wait_ge(s_dn, n * ST + i + 1 + ONE)
                    a1 = acc[:, bass.ds(g * ST + i, 1)].rearrange("p o e -> p (o e)")
                    c1 = comb[:, bass.ds(g * ST + i, 1), bass.ds(e, 1)].rearrange("p a b -> p (a b)")
                    nc.vector.scalar_tensor_tensor(a1, dn[i % 2][:, 0:E], c1, a1, ALU.mult, ALU.add).then_inc(s_y, 1)

            steps(dve, body)
            dve.wait_ge(s_y, NE * NT + ONE)

        @block.tensor
        def _(pe):
            def body(e, e2, par, half, gi):
                n = number(e, half, gi)
                tab = (tabq, tabk)[half]
                first = pe.snap((S - 1) - e * LB - gi * RU)
                pe.wait_ge(s_w[par], e2 * 32 + 32 + ONE)
                pe.wait_ge(s_st[half], (e + 1) * 16 * len(PAIRS) + ONE)
                for f in range(FC):
                    if f >= 2:
                        pe.wait_ge(s_h, n * FC + f - 1 + ONE)
                    for k in range(KC):
                        last = nc.tensor.matmul(up[f % 2][:], w1[par][:, k, f * P:(f + 1) * P],
                                                tok[:, bass.ds(gi + half * GH, 1), k].rearrange("p o s -> p (o s)"), start=(k == 0), stop=(k == KC - 1))
                    last.then_inc(s_up, 1)
                    who = (s_ra, s_rv)[f % 2]
                    wait(pe, who, n * 4 + f // 2)
                    for u in range(2):
                        i = gi * RU + (f * 2 + u)
                        lhs = stack[half][:, :, bass.ds(i, 1)].rearrange("p h o -> p (h o)")
                        rhs = tab[:, bass.ds(first - (f * 2 + u), S)]
                        last = nc.tensor.matmul(rl[f % 2][:, u], lhs, rhs, start=True, stop=True)
                    last.then_inc(s_rm, 1)
                for i in range(ST):
                    wait(pe, s_y, n * ST + max(i - 1, 0))
                    for f in range(FC):
                        if i == 0:
                            pe.wait_ge(s_h, n * FC + f + 1 + ONE)
                        last = nc.tensor.matmul(dn[i % 2][:, 0:E], hid[:, f, i * P:(i + 1) * P], w2[par][:, f],
                                                start=(f == 0), stop=(f == FC - 1))
                    last.then_inc(s_dn, 1)

            pe.wait_ge(s_tok, 16)
            steps(pe, body)


def attention(nc, t, keep):
    with ExitStack() as ctx:
        def sb(name, shape, dt=F32):
            return ctx.enter_context(nc.sbuf_tensor(name, shape, dt))

        sems = []

        def sem(name):
            sems.append(ctx.enter_context(nc.semaphore(name)))
            return sems[-1]

        def dma_sem(name):
            return ctx.enter_context(nc.semaphore(name))

        ident, acc = keep["ident"], keep["acc"]
        HG = 4
        NG = H // HG
        sc = [ctx.enter_context(nc.psum_tensor(f"sc{i}", [P, S], F32)) for i in range(2)]
        pt = [ctx.enter_context(nc.psum_tensor(f"pt{i}", [P, S], F32)) for i in range(2)]
        cx = [ctx.enter_context(nc.psum_tensor(f"cx{i}", [P, S], F32)) for i in range(2)]
        wo_ps = [ctx.enter_context(nc.psum_tensor(f"wo_ps{i}", [P, S], F32)) for i in range(2)]
        wo = sb("wo_sb", [P, NG, E])
        sel = sb("sel", [P, P])
        gb = sb("gamma_beta", [P, 2, E])
        rq = [sb(f"rq{i}", [P, ST, S]) for i in range(2)]
        rk = [sb(f"rk{i}", [P, ST, S]) for i in range(2)]
        qs = [sb(f"qs{i}", [KS, HG, S], BF16) for i in range(2)]
        ks = [sb(f"ks{i}", [KS, HG, S], BF16) for i in range(2)]
        vs = [sb(f"vs{i}", [P, ST, HG * DA]) for i in range(2)]
        sm = sb("scores", [P, 2, ST, S])
        mx = sb("row_max", [P, 2, ST])
        nb = sb("neg_max", [P, 2, ST])
        pT = sb("probsT", [P, HG, ST, S])
        cs = sb("ctx_raw", [P, S])
        rc = sb("ctx_recip", [P, S])
        cT = sb("ctxT", [P, NG, S])
        xo = sb("xo", [P, ST, E])
        xx = sb("xx", [P, ST, E])
        hh = sb("hh", [P, ST, E])
        oo = sb("oo", [P, ST, E])
        stats = sb("att_stats", [P, ST, 6]), sb("att_mv", [P, ST, 2]), sb("att_work", [P, 3, ST])

        s_const = sem("consts_loaded")
        s_rq = [sem(f"rq_loaded{i}") for i in range(2)]
        s_rk = [sem(f"rk_loaded{i}") for i in range(2)]
        s_qkv = [sem(f"qkv_loaded{i}") for i in range(2)]
        s_zero = sem("ctx_zeroed")
        s_sc, s_su = sem("scores_done"), sem("scores_taken")
        s_d = sem("dve_max_steps")
        s_nb, s_e = sem("neg_max_ready"), sem("exp_done")
        s_pt, s_pa, s_pd = sem("probs_turned"), sem("probsT_by_act"), sem("probsT_by_dve")
        s_pv, s_cs, s_bc, s_n = sem("ctx_done"), sem("ctx_copied"), sem("sums_spread"), sem("norm_steps")
        s_wo, s_h, s_f = sem("wo_done"), sem("out_norm_steps"), sem("final_steps")
        s_xl, s_g, s_out = dma_sem("x_reloaded"), sem("gate_ready"), dma_sem("out_stored")
        RQ0 = ST
        PV0 = 1
        F_STEPS = 6
        NQKV = 2 * len(PAIRS) + 1
        spare = sb("att_spare", [P, ST + 1])
        pad = sb("pool_spare", [P, 2])
        s_pad = sem("pool_spare_set")

        start_at_one(nc, sems, [(s_sc, RQ0), (s_su, RQ0), (s_pv, PV0)])
        block = ctx.enter_context(nc.Block())

        @block.sync
        def _(sp):
            sp.dma_start(wo[:], t["wo"]).then_inc(s_const, 16)
            sp.dma_start(sel[:], t["sel"]).then_inc(s_const, 16)
            sp.dma_start(gb[:], t["vecs"][VECS.index("ln_gamma"):VECS.index("ln_beta") + 1].partition_broadcast(P)).then_inc(s_const, 16)
            with sp.Fori(0, B) as b:
                for hg in range(NG):
                    i = hg % 2
                    sp.wait_ge(s_pv, b * NG + (hg - 1 + PV0) + ONE)
                    for dst, name, side in ((qs, "qparts", 0), (ks, "kparts", 1)):
                        for n, pair in enumerate(PAIRS):
                            src = t[name][pair[side], bass.ds(b, 1)].rearrange("o (h d) s -> d (o h) s", d=D)
                            sp.dma_start(dst[i][n * D:(n + 1) * D], src[:, hg * HG:(hg + 1) * HG]).then_inc(s_qkv[i], 16)
                    src = t["va"][bass.ds(b * S, S)].rearrange("(t p) h d -> p t (h d)", p=P)
                    sp.dma_start(vs[i][:], src[:, :, hg * HG * DA:(hg + 1) * HG * DA]).then_inc(s_qkv[i], 16)
                    for j in range(HG):
                        n = b * H + (hg * HG + j)
                        sp.wait_ge(s_sc, n * ST + ONE)
                        sp.wait_ge(s_su, n * ST + ONE)
                        for dst, name, done in ((rk, "relk", s_rk), (rq, "relq", s_rq)):
                            src = t[name][bass.ds(n, 1), 0:S * S].rearrange("o (t p s) -> p (o t) s", p=P, s=S)
                            sp.dma_start(dst[j % 2][:], src).then_inc(done[j % 2], 16)

        @block.gpsimd
        def _(pool):
            nc.gpsimd.memset(pad[:, 0:1], 0.0).then_inc(s_pad, 1)
            pool.wait_ge(s_pad, 1 + ONE)
            pool.wait_ge(s_const, 48 + ONE)
            with pool.Fori(0, B) as b:
                pool.wait_ge(s_f, b * F_STEPS + ONE)
                pool.dma_start(xo[:], t["xnbo"][bass.ds(b * S, S)].rearrange("(t p) e -> p t e", p=P)).then_inc(s_xl, 16)
                pool.dma_start(xx[:], t["x"][bass.ds(b * S, S)].rearrange("(t p) e -> p t e", p=P)).then_inc(s_xl, 16)
                step = Steps(pool, s_f, b * F_STEPS)
                pool.wait_ge(s_h, (b + 1) * (2 + NORM_STEPS) + ONE)
                step.did(nc.gpsimd.tensor_tensor(oo[:], oo[:], over_tiles(gb[:, 0], ST), ALU.mult))
                step.settle()
                step.did(nc.gpsimd.tensor_tensor(oo[:], oo[:], over_tiles(gb[:, 1], ST), ALU.add))
                step.settle()
                pool.wait_ge(s_g, b + 1 + ONE)
                step.did(nc.gpsimd.tensor_tensor(oo[:], oo[:], acc[:, bass.ds(b * ST, ST)], ALU.mult))
                step.settle()
                step.did(nc.gpsimd.tensor_tensor(oo[:], oo[:], xx[:], ALU.add))
                step.settle()
                step.did(nc.gpsimd.tensor_tensor(pad[:, 1:2], pad[:, 0:1], pad[:, 0:1], ALU.add))
                pool.dma_start(t["out"][bass.ds(b * S, S)].rearrange("(t p) e -> p t e", p=P), oo[:]).then_inc(s_out, 16)
                step.settle()
                pool.wait_ge(s_out, (b + 1) * 16)
                step.did(nc.gpsimd.tensor_tensor(pad[:, 1:2], pad[:, 0:1], pad[:, 0:1], ALU.add))
            pool.wait_ge(s_out, 16 * B)


        def rounds(eng, score, rest, after_batch):
            score(0, 0, 0, 0)

            def batch(b, last):
                for h in range(H):
                    hg, j = h // HG, h % HG
                    if h < H - 1:
                        score(b, h + 1, (h + 1) // HG, (h + 1) % HG)
                    elif not last:
                        score(b + 1, 0, 0, 0)
                    rest(b, h, hg, j)
                after_batch(b)

            with eng.Fori(0, B - 1) as b:
                batch(b, False)
            batch(B - 1, True)

        @block.scalar
        def _(act):
            def score(b, h, hg, j):
                head = b * H + h
                for i in range(ST):
                    act.wait_ge(s_nb, head + 1 + ONE)
                    nc.scalar.activation(sm[:, j % 2, i], sm[:, j % 2, i], ACT.Exp, bias=nb[:, j % 2, i:i + 1],
                                         scale=SM_SCALE).then_inc(s_e, 1)

            def rest(b, h, hg, j):
                head = b * H + h
                for i in range(0, ST, 2):
                    act.wait_ge(s_pt, head * ST + i + 1 + ONE)
                    nc.scalar.copy(pT[:, j, i], pt[0][:]).then_inc(s_pa, 1)

            def gate(b):
                nc.scalar.activation(acc[:, bass.ds(b * ST, ST)], acc[:, bass.ds(b * ST, ST)], ACT.Silu).then_inc(s_g, 1)

            def batch(b, last):
                for h in range(H):
                    rest(b, h, h // HG, h % HG)
                    if h < H - 1:
                        score(b, h + 1, (h + 1) // HG, (h + 1) % HG)
                    elif not last:
                        score(b + 1, 0, 0, 0)
                gate(b)

            score(0, 0, 0, 0)
            with act.Fori(0, B - 1) as b:
                batch(b, False)
            batch(B - 1, True)

        @block.vector
        def _(dve):
            for i in range(2):
                nc.vector.memset(cx[i][:], 0.0).then_inc(s_zero, 1)

            def score(b, h, hg, j):
                head = b * H + h
                step = Steps(dve, s_d, head * ST)
                dve.wait_ge(s_rq[j % 2], (b * (H // 2) + (h // 2 + 1)) * 16 + ONE)
                wait(dve, s_pt, (head - 1) * ST)
                for i in range(ST):
                    dve.wait_ge(s_sc, head * ST + (i + 1 + RQ0) + ONE)
                    nc.vector.memset(spare[:, i:i + 1], 0.0)
                    nc.vector.tensor_tensor_reduce(sm[:, j % 2, i], sc[i % 2][:], rq[j % 2][:, i], 1.0, -3.0e38,
                                                   ALU.add, ALU.max, mx[:, j % 2, i:i + 1]).then_inc(s_su, 1)
                dve.wait_ge(s_su, head * ST + (ST + RQ0) + ONE)
                nc.vector.tensor_scalar(nb[:, j % 2], mx[:, j % 2], -SM_SCALE, None, ALU.mult).then_inc(s_nb, 1)

            def rest(b, h, hg, j):
                head = b * H + h
                for i in range(1, ST, 2):
                    dve.wait_ge(s_pt, head * ST + i + 1 + ONE)
                    nc.vector.tensor_copy(pT[:, j, i], pt[1][:]).then_inc(s_pd, 1)
                if j == HG - 1:
                    group = b * NG + hg
                    step = Steps(dve, s_n, group * 2)
                    dve.wait_ge(s_pv, group + (1 + PV0) + ONE)
                    nc.vector.tensor_copy(cs[:], cx[hg % 2][:]).then_inc(s_cs, 1)
                    dve.wait_ge(s_bc, group + 1 + ONE)
                    step.did(nc.vector.reciprocal(rc[:], wo_ps[0][:]))
                    step.settle()
                    dve.wait_ge(s_wo, b * 2 + ONE)
                    step.did(nc.vector.tensor_tensor(cT[:, hg], cs[:], rc[:], ALU.mult))

            def after_batch(b):
                step = Steps(dve, s_h, b * (2 + NORM_STEPS), spare[:, ST:ST + 1])
                dve.wait_ge(s_xl, (b + 1) * 32)
                for i in range(2):
                    dve.wait_ge(s_wo, b * 2 + i + 1 + ONE)
                    step.did(nc.vector.tensor_tensor(hh[:, 2 * i:2 * i + 2], wo_ps[i][:].rearrange("p (t e) -> p t e", t=2),
                                                     xo[:, 2 * i:2 * i + 2], ALU.add))
                step.settle()
                dve.wait_ge(s_f, b * F_STEPS + ONE)
                normalize(nc, step, hh, oo, EPS_ATT, stats)

            rounds(dve, score, rest, after_batch)

        @block.tensor
        def _(pe):
            pe.wait_ge(s_const, 48 + ONE)
            pe.wait_ge(s_zero, 2 + ONE)

            def score(b, h, hg, j):
                head = b * H + h
                g2 = hg % 2
                pe.wait_ge(s_rk[j % 2], (b * (H // 2) + (h // 2 + 1)) * 16 + ONE)
                if j == 0:
                    pe.wait_ge(s_qkv[g2], (b * 2 + (hg // 2 + 1)) * (16 * NQKV) + ONE)
                for i in range(ST):
                    if not (isinstance(head, int) and head == 0 and i < 2):
                        pe.wait_ge(s_su, head * ST + (i - 1 + RQ0) + ONE)
                    for r in range(ST):
                        nc.tensor.matmul(sc[i % 2][:, r * P:(r + 1) * P], rk[j % 2][:, r, i * P:(i + 1) * P], ident[:],
                                         start=(r == 0), stop=False, is_transpose=True, skip_group_check=True)
                    nc.tensor.matmul(sc[i % 2][:], qs[g2][:, j, i * P:(i + 1) * P], ks[g2][:, j], start=False,
                                     stop=True, skip_group_check=True).then_inc(s_sc, 1)

            def rest(b, h, hg, j):
                head = b * H + h
                pe.wait_ge(s_e, (head + 1) * ST + ONE)
                for r in range(ST):
                    who, at = (s_pa, s_pd)[r % 2], head * (ST // 2) + r // 2
                    wait(pe, who, at)
                    for i in range(ST):
                        last = nc.tensor.transpose(pt[r % 2][:, i * P:(i + 1) * P], sm[:, j % 2, i, r * P:(r + 1) * P], ident[:])
                    last.then_inc(s_pt, 1)
                if j == HG - 1:
                    group = b * NG + hg
                    pe.wait_ge(s_pa, (head + 1) * (ST // 2) + ONE)
                    pe.wait_ge(s_pd, (head + 1) * (ST // 2) + ONE)
                    if hg > 0:
                        pe.wait_ge(s_n, (group - 1) * 2 + ONE)
                    for r in range(ST):
                        for k in range(HG):
                            last = nc.tensor.matmul(cx[hg % 2][32 * k:32 * k + DA], vs[hg % 2][:, r, k * DA:(k + 1) * DA],
                                                    pT[:, k, r], start=(r == 0), stop=(r == ST - 1), skip_group_check=True)
                    last.then_inc(s_pv, 1)
                    pe.wait_ge(s_cs, group + 1 + ONE)
                    if hg == 0:
                        pe.wait_ge(s_h, b * (2 + NORM_STEPS) + ONE)
                    else:
                        pe.wait_ge(s_n, group * 2 + ONE)
                    nc.tensor.matmul(wo_ps[0][:], sel[:], cs[:], start=True, stop=True).then_inc(s_bc, 1)

            def after_batch(b):
                pe.wait_ge(s_n, (b + 1) * (NG * 2) + ONE)
                for i in range(ST):
                    for k in range(NG):
                        last = nc.tensor.matmul(wo_ps[i // 2][:, (i % 2) * E:(i % 2 + 1) * E], cT[:, k, i * P:(i + 1) * P],
                                                wo[:, k], start=(k == 0), stop=(k == NG - 1), skip_group_check=True)
                    if i % 2:
                        last.then_inc(s_wo, 1)

            rounds(pe, score, rest, after_batch)


def program(nc, t):
    with ExitStack() as ctx:
        def sb(name, shape, dt=F32):
            return ctx.enter_context(nc.sbuf_tensor(name, shape, dt))

        keep = {
            "ident": sb("ident", [P, P]),
            "acc": sb("acc", [P, NT, E]),
            "comb": sb("comb", [P, NT, NE]),
            "tabq": sb("tabq", [KS, WIN], BF16),
            "tabk": sb("tabk", [KS, WIN], BF16),
        }
        prep(nc, t, keep)
        experts(nc, t, keep)
        attention(nc, t, keep)


def kernel(**inputs):
    import numpy as np
    import concourse.bacc as bacc
    from concourse.bass_utils import run_bass_kernel_spmd

    a = {n: np.ascontiguousarray(v) for n, v in inputs.items()}
    x = a["L0_attn_hidden_states"]
    emb = a["L0_attn_dist_emb"]
    dist = S - 1 - np.arange(WIN)
    row = dist + M_POS - 1
    row = np.where(row < 0, row + emb.shape[0], row)
    row = np.clip(row, 0, emb.shape[0] - 1)
    tabq = emb[row].T
    tabk = np.concatenate([tabq[:, WIN - 2::-1], tabq[:, :1]], axis=1)
    wo = np.zeros((H // 4, 4, 32, E), np.float32)
    wo[:, :, :D] = a["L0_attn_Wo"].reshape(H // 4, 4, D, E)
    sel = np.zeros((P, P), np.float32)
    for g in range(4):
        sel[32 * g + D, 32 * g:32 * (g + 1)] = 1.0
    mask = np.array([[-(p[1] > 0), -(p[1] > 1)] for p in PAIRS], np.float32).repeat(D, axis=0)
    f = {"bv": "L0_attn_bv", "bo": "L0_attn_bo", "mix_b": "L0_ffn_mix_b", "g1": "L0_ffn_g1", "be1": "L0_ffn_be1",
         "g2": "L0_ffn_g2", "be2": "L0_ffn_be2", "ln_gamma": "L0_attn_ln_gamma", "ln_beta": "L0_attn_ln_beta"}
    arrays = {
        "x": x.reshape(B * S, E),
        "Wq": a["L0_attn_Wq"], "Wk": a["L0_attn_Wk"], "Wv": a["L0_attn_Wv"],
        "mix_w": a["L0_ffn_mix_w"], "router_w": a["L0_ffn_router_w"],
        "wo": wo.reshape(H // 4, P, E).transpose(1, 0, 2),
        "w1": a["L0_ffn_w1"], "w2": a["L0_ffn_w2"],
        "b1": a["L0_ffn_b1"].reshape(NE, FC, P).transpose(2, 0, 1),
        "b2": a["L0_ffn_b2"],
        "bqk": np.stack([a["L0_attn_bq"], a["L0_attn_bk"]]).reshape(2 * KC, P).T,
        "vecs": np.stack([a[f[n]] for n in VECS]),
        "tabq": np.tile(tabq, (len(PAIRS), 1)), "tabk": np.tile(tabk, (len(PAIRS), 1)),
        "mask": mask, "sel": sel, "ident": np.eye(P, dtype=np.float32),
    }
    nc = bacc.Bacc("TRN2", target_bir_lowering=False, num_devices=1)
    t, ins = {}, {}
    for name, v in arrays.items():
        v = np.ascontiguousarray(v)
        ins[f"in_{name}"] = v
        t[name] = nc.dram_tensor(f"in_{name}", v.shape, mybir.dt.from_np(v.dtype), kind="ExternalInput").ap()
    for name, shape, dt in (("qparts", (PARTS, B, E, S), BF16), ("kparts", (PARTS, B, E, S), BF16),
                            ("xnbo", (B * S, E), F32), ("va", (B * S, H, DA), F32), ("flatT", (B * P, KC, S), F32),
                            ("relq", (BH, PITCH), F32), ("relk", (BH, PITCH), F32)):
        t[name] = nc.dram_tensor(f"scratch_{name}", shape, dt).ap()
    t["out"] = nc.dram_tensor("out_0", (B * S, E), F32, kind="ExternalOutput").ap()
    program(nc, t)
    got = run_bass_kernel_spmd(nc, [ins], core_ids=[0])
    return got.results[0]["out_0"].reshape(B, S, E)
```

```python
from contextlib import ExitStack

import concourse.bass as bass
from concourse import mybir

F32 = mybir.dt.float32
BF16 = mybir.dt.bfloat16
I32 = mybir.dt.int32
FR = mybir.dt.float32r
ALU = mybir.AluOpType
ACT = mybir.ActivationFunctionType
AX = mybir.AxisListType

P = 128
B, S, E = 8, 512, 256
H, D = 16, 16
M_POS = 256
NE, F = 8, 1024
TOPK = 2
BH = B * H
ST = S // P
NT = B * ST
KC = E // P
FC = F // P
PARTS = 3
PAIRS = [(0, 0), (0, 1), (1, 0), (1, 1), (0, 2), (2, 0)]
KS = D * len(PAIRS)
WIN = 2 * S
LB = 64
RU = 16
PITCH = S * S + 1024
ONE = 1
EPS_LN, EPS_ATT = 1e-5, 1e-12
SM_SCALE = float(D) ** -0.5
VECS = ["bv", "bo", "mix_b", "g1", "be1", "g2", "be2", "ln_gamma", "ln_beta"]


def start_at_one(nc, sems, free=()):
    with nc.Block() as block:
        @block.gpsimd
        def _(pool):
            for s in sems:
                pool.sem_inc(s, ONE)
            for s, n in free:
                pool.sem_inc(s, n)


def wait(eng, sem, value):
    if isinstance(value, int) and value <= 0:
        return
    eng.wait_ge(sem, value + ONE)


class Steps:

    def __init__(self, eng, sem, base, spare=None):
        self.eng, self.sem, self.base, self.n, self.spare = eng, sem, base, 0, spare

    def did(self, ins):
        ins.then_inc(self.sem, 1)
        self.n += 1

    def settle(self):
        wait(self.eng, self.sem, self.base + self.n)

    def settle_apart(self):
        self.settle()
        self.eng.memset(self.spare, 0.0)


def paired(eng, n, first, second):
    first(0, 0)
    with eng.Fori(0, (n - 2) // 2) as i:
        first(i * 2 + 1, 1)
        second(i * 2, 0)
        first(i * 2 + 2, 0)
        second(i * 2 + 1, 1)
    first(n - 1, 1)
    second(n - 2, 0)
    second(n - 1, 1)


def over_tiles(vec, n):
    return vec.unsqueeze(1).to_broadcast([P, n, E])


def inverse_sqrt(nc, step, var, eps, work):
    ve, a, y = (work[:, i] for i in range(3))
    step.did(nc.vector.tensor_scalar(ve, var, eps, None, ALU.add))
    step.settle()
    step.did(nc.vector.tensor_scalar(a.bitcast(I32), ve.bitcast(I32), 1, None, ALU.logical_shift_right))
    step.settle()
    step.did(nc.vector.tensor_scalar(y.bitcast(I32), a.bitcast(I32), -1, 0x5F3759DF, ALU.mult, ALU.add))
    step.settle()
    for _ in range(3):
        step.did(nc.vector.tensor_tensor(a, y, y, ALU.mult))
        step.settle()
        step.did(nc.vector.tensor_tensor(a, a, ve, ALU.mult))
        step.settle()
        step.did(nc.vector.tensor_scalar(a, a, -0.5, 1.5, ALU.mult, ALU.add))
        step.settle()
        step.did(nc.vector.tensor_tensor(y, y, a, ALU.mult))
        step.settle()


NORM_STEPS = 3 * ST + 15


def normalize(nc, step, src, dst, eps, stats):
    st, mv, work = stats
    for i in range(ST):
        step.did(nc.vector.bn_stats(st[:, i], src[:, i]))
    step.settle_apart()
    for i in range(ST):
        step.did(nc.vector.bn_aggr(mv[:, i], st[:, i]))
    step.settle()
    inverse_sqrt(nc, step, mv[:, :, 1], eps, work)
    for i in range(ST):
        step.did(nc.vector.tensor_scalar(dst[:, i], src[:, i], mv[:, i, 0:1], work[:, 2, i:i + 1], ALU.subtract, ALU.mult))
    step.settle()


def prep(nc, t, keep):
    with ExitStack() as ctx:
        def sb(name, shape, dt=F32):
            return ctx.enter_context(nc.sbuf_tensor(name, shape, dt))

        sems = []

        def sem(name):
            sems.append(ctx.enter_context(nc.semaphore(name)))
            return sems[-1]

        def dma_sem(name):
            return ctx.enter_context(nc.semaphore(name))

        ident = keep["ident"]
        acc, comb, tabq, tabk = keep["acc"], keep["comb"], keep["tabq"], keep["tabk"]
        bank = [ctx.enter_context(nc.psum_tensor(f"prep_bank{i}", [P, 512], F32)) for i in range(8)]
        vec = sb("vecs", [P, len(VECS), E])
        V = {n: vec[:, i, :] for i, n in enumerate(VECS)}
        wq, wk, wv, mix = (sb(n, [P, KC, E]) for n in ("wq_sb", "wk_sb", "wv_sb", "mix_sb"))
        rw = sb("router_sb", [P, KC, NE])
        b2 = sb("b2_sb", [NE, E])
        bqk = sb("bqk_sb", [P, 4])
        mask = sb("mask_sb", [KS, 2])
        tab32 = sb("tab32", [KS, 2, WIN])
        tmp32 = sb("tmp32", [KS, WIN])
        tabh = sb("tabh", [KS, WIN], BF16)
        xs = sb("xs", [P, 2, ST, E])
        xn = sb("xn", [P, 2, ST, E])
        n1 = sb("n1", [P, 2, ST, E])
        n1r = sb("n1r", [P, ST, E])
        xb = sb("xn_plus_bo", [P, ST, E])
        xm = sb("xn_plus_mixb", [P, 2, ST, E])
        stats1, stats2 = ((sb(f"bn_stats{i}", [P, ST, 6]), sb(f"bn_mv{i}", [P, ST, 2]), sb(f"bn_work{i}", [P, 3, ST]))
                          for i in range(2))
        xnT = sb("xnT", [P, 2, KC, S])
        n1T = sb("n1T", [P, 2, KC, S])
        qk32 = sb("qk32", [P, 4, S])
        qkr = sb("qkr", [P, 4, S])
        part = [sb(f"part{i}", [P, 4, S], BF16) for i in range(PARTS)]
        va = sb("va", [P, ST, E])
        zero = sb("zero", [P, 1])
        s_zero = sem("zero_set")
        n2 = sb("n2", [P, ST, E])
        n2T = sb("n2T", [P, KC, S])
        pr = sb("probs8", [P, ST, NE])
        rest = sb("rest8", [P, ST, NE])
        top = sb("top8", [P, ST, 8])
        m8 = sb("m8", [P, ST, 1])
        cb = sb("cb", [P, ST, NE])
        cT = sb("cT", [NE, S])
        raw, high, low = (sb(n, [P, KC * F]) for n in ("raw", "high", "low"))
        n2h, n2l = sb("n2T_high", [P, KC, S]), sb("n2T_low", [P, KC, S])
        s_ld, s_hi, s_lo, s_wst = sem("raw_loaded"), sem("high_ready"), sem("low_ready"), sem("weights_out")
        s_th, s_tl = sem("tokens_high"), sem("tokens_low")

        def weight_turn(g, is_first):
            if is_first:
                return (0, 0, 0) if isinstance(g, int) and g == 0 else (g * 2 - 1, 1, g - 1)
            return (2 * NE - 1, 1, NE - 1) if isinstance(g, int) and g == B - 1 else (g * 2 + 2, 0, g + 1)

        s_const, s_xb_st, s_va_st, s_n2_st, s_part_st = (sem(n) for n in (
            "const_loaded", "xb_stored", "va_stored", "n2T_stored", "parts_stored"))
        s_x = [sem(f"x_loaded{i}") for i in range(2)]
        s_tab = sem("tab_steps")
        s_d1, s_d2, s_d3 = sem("dve_first"), sem("dve_second"), sem("dve_router")
        s_xn, s_n1 = sem("xn_ready"), sem("n1_ready")
        s_pool = sem("pool_steps")
        s_tx, s_tn, s_qkp, s_vmp = sem("xn_turned"), sem("n1_turned"), sem("qk_product"), sem("vmix_product")
        s_cx, s_cn, s_qk = sem("xnT_copied"), sem("n1T_copied"), sem("qk_copied")
        s_vu, s_mu = sem("v_taken"), sem("mix_taken")
        s_n2, s_t2, s_c2, s_lg = sem("n2_ready"), sem("n2_turned"), sem("n2T_copied"), sem("logits_ready")
        s_sh, s_ex, s_cb = sem("logits_shifted"), sem("exp8_done"), sem("comb_ready")
        s_ct, s_cc, s_b2p, s_b2u = sem("comb_turned"), sem("combT_copied"), sem("b2_product"), sem("b2_added")
        NCONST = 12
        POOL_N = 6
        spare = sb("spare", [P, 1])

        start_at_one(nc, sems)
        block = ctx.enter_context(nc.Block())

        @block.sync
        def _(sp):
            sp.dma_start(ident[:], t["ident"]).then_inc(s_const, 16)
            for dst, src in ((wq, "Wq"), (wk, "Wk"), (wv, "Wv"), (mix, "mix_w"), (rw, "router_w")):
                sp.dma_start(dst[:], t[src].rearrange("(k p) n -> p k n", p=P)).then_inc(s_const, 16)
            sp.dma_start(vec[:], t["vecs"].partition_broadcast(P)).then_inc(s_const, 16)
            sp.dma_start(b2[:], t["b2"]).then_inc(s_const, 16)
            sp.dma_start(bqk[:], t["bqk"]).then_inc(s_const, 16)
            sp.dma_start(mask[:], t["mask"]).then_inc(s_const, 16)
            for i, name in enumerate(("tabq", "tabk")):
                sp.dma_start(tab32[:, i], t[name]).then_inc(s_const, 16)

            def load_weight(which, e):
                src = t[("w1", "w2")[which]][bass.ds(e, 1)].rearrange("o (k p) f -> p (o k) f", p=P)
                sp.dma_start(raw[:].rearrange("p (k f) -> p k f", k=(KC, FC)[which]), src).then_inc(s_ld, 16)

            def weight(g, is_first):
                n, which, e = weight_turn(g, is_first)
                sp.wait_ge(s_lo, n + 1 + ONE)
                for a, src in enumerate((high, low)):
                    sp.dma_start(t[("w1s", "w2s")[which]][a, bass.ds(e * P, P)], src[:]).then_inc(s_wst, 16)
                if not (isinstance(n, int) and n == 2 * NE - 1):
                    load_weight(1 - which, e + which)

            def load(g, par):
                wait(sp, s_xn, g - 1)
                sp.dma_start(xs[:, par], t["x"][bass.ds(g * S, S)].rearrange("(t p) e -> p t e", p=P)).then_inc(s_x[par], 16)

            def store(g, par):
                sp.wait_ge(s_pool, g * POOL_N + 1 + ONE)
                sp.dma_start(t["xnbo"][bass.ds(g * S, S)].rearrange("(t p) e -> p t e", p=P), xb[:]).then_inc(s_xb_st, 16)
                sp.wait_ge(s_pool, g * POOL_N + POOL_N + ONE)
                for i in range(PARTS):
                    for c in range(4):
                        dst = (t["qparts"], t["kparts"])[c // 2]
                        dst = dst[i, bass.ds(g, 1)].rearrange("o (c p) s -> (o c) p s", c=2)[c % 2]
                        sp.dma_start(dst, part[i][:, c]).then_inc(s_part_st, 16)
                sp.wait_ge(s_vu, (g + 1) * ST + ONE)
                sp.dma_start(t["va"][bass.ds(g * S, S)].rearrange("(t p) e -> p t e", p=P), va[:]).then_inc(s_va_st, 16)

            def second(g, par):
                sp.wait_ge(s_tl, g + 1 + ONE)
                for a, src in enumerate((n2h, n2l)):
                    sp.dma_start(t["toks"][a, bass.ds(g * P, P)], src[:].rearrange("p k s -> p (k s)")).then_inc(s_n2_st, 16)
                weight(g, False)

            def first(g, par):
                if not (isinstance(g, int) and g == B - 1):
                    load(g + 1, 1 - par)
                store(g, par)
                weight(g, True)

            load(0, 0)
            load_weight(0, 0)

            paired(sp, B, first, second)
            sp.wait_ge(s_xb_st, 16 * B + ONE)
            sp.wait_ge(s_part_st, 16 * B * PARTS * 4 + ONE)
            sp.wait_ge(s_va_st, 16 * B + ONE)
            sp.wait_ge(s_n2_st, 32 * B + ONE)
            sp.wait_ge(s_wst, 64 * NE + ONE)

        @block.gpsimd
        def _(pool):
            nc.gpsimd.memset(zero[:], 0.0).then_inc(s_zero, 1)
            pool.wait_ge(s_zero, 1 + ONE)
            zeros = zero[:].unsqueeze(2).to_broadcast([P, 4, S])
            pool.wait_ge(s_const, 16 * NCONST + ONE)

            def first(g, par):
                step = Steps(pool, s_pool, g * POOL_N)
                pool.wait_ge(s_xn, g + 1 + ONE)
                wait(pool, s_xb_st, 16 * g)
                step.did(nc.gpsimd.tensor_tensor(xb[:], xn[:, par], over_tiles(V["bo"], ST), ALU.add))
                wait(pool, s_n2, g - 1)
                step.did(nc.gpsimd.tensor_tensor(xm[:, par], xn[:, par], over_tiles(V["mix_b"], ST), ALU.add))
                pool.wait_ge(s_qk, 4 * (g + 1) + ONE)
                wait(pool, s_part_st, 16 * PARTS * 4 * g)
                step.did(nc.gpsimd.tensor_tensor(part[0][:], qk32[:], zeros, ALU.add))
                step.settle()
                step.did(nc.gpsimd.tensor_tensor(qkr[:], qk32[:], part[0][:], ALU.subtract))
                step.settle()
                step.did(nc.gpsimd.tensor_tensor(part[1][:], qkr[:], zeros, ALU.add))
                step.settle()
                step.did(nc.gpsimd.tensor_tensor(part[2][:], qkr[:], part[1][:], ALU.subtract))
                weight(g, True)

            def weight(g, is_first):
                n, which, e = weight_turn(g, is_first)
                pool.wait_ge(s_hi, n + 1 + ONE)
                nc.gpsimd.tensor_tensor(low[:].bitcast(FR), raw[:], high[:], ALU.subtract).then_inc(s_lo, 1)

            def second(g, par):
                pool.wait_ge(s_th, g + 1 + ONE)
                nc.gpsimd.tensor_tensor(n2l[:].bitcast(FR), n2T[:], n2h[:], ALU.subtract).then_inc(s_tl, 1)
                weight(g, False)

            paired(pool, B, first, second)

        @block.scalar
        def _(act):
            act.wait_ge(s_const, 16 * NCONST + ONE)

            def first(g, par):
                for k in range(KC):
                    act.wait_ge(s_tx, (g * KC) + k + 1 + ONE)
                    nc.scalar.copy(xnT[:, par, k], bank[k][:]).then_inc(s_cx, 1)
                wait(act, s_pool, g * POOL_N)
                for c in range(4):
                    act.wait_ge(s_qkp, g * 4 + c + 1 + ONE)
                    nc.scalar.activation(qk32[:, c], bank[4 + c % 2][:], ACT.Identity, bias=bqk[:, c:c + 1]).then_inc(s_qk, 1)
                for k in range(KC):
                    act.wait_ge(s_tn, (g * KC) + k + 1 + ONE)
                    nc.scalar.copy(n1T[:, par, k], bank[2 + k][:]).then_inc(s_cn, 1)
                weight(g, True)

            def weight(g, is_first):
                n, which, e = weight_turn(g, is_first)
                act.wait_ge(s_ld, n * 16 + 16 + ONE)
                act.wait_ge(s_wst, n * 32 + ONE)
                nc.scalar.copy(high[:].bitcast(FR), raw[:]).then_inc(s_hi, 1)

            def second(g, par):
                wait(act, s_n2_st, 32 * g)
                for k in range(KC):
                    act.wait_ge(s_t2, g * KC + k + 1 + ONE)
                    nc.scalar.copy(n2T[:, k], bank[k][:]).then_inc(s_c2, 1)
                act.wait_ge(s_c2, (g + 1) * KC + ONE)
                nc.scalar.copy(n2h[:].bitcast(FR), n2T[:]).then_inc(s_th, 1)
                act.wait_ge(s_sh, g + 1 + ONE)
                nc.scalar.activation(pr[:], pr[:], ACT.Exp).then_inc(s_ex, 1)
                act.wait_ge(s_ct, g + 1 + ONE)
                nc.scalar.copy(cT[:], bank[3][0:NE, :]).then_inc(s_cc, 1)
                weight(g, False)

            paired(act, B, first, second)

        @block.vector
        def _(dve):
            dve.wait_ge(s_const, 16 * NCONST + ONE)
            tab = Steps(dve, s_tab, 0)

            def split_table(dst, i):
                tab.did(nc.vector.tensor_copy(tabh[:], tab32[:, i]))
                tab.settle()
                tab.did(nc.vector.scalar_tensor_tensor(tmp32[:], tabh[:], mask[:, 0:1], tab32[:, i], ALU.mult, ALU.add))
                tab.settle()
                tab.did(nc.vector.tensor_copy(tabh[:], tmp32[:]))
                tab.settle()
                tab.did(nc.vector.scalar_tensor_tensor(dst[:], tabh[:], mask[:, 1:2], tmp32[:], ALU.mult, ALU.add))

            split_table(tabq, 0)
            tab.settle()
            split_table(tabk, 1)
            tab.settle()
            D1 = 2 * NORM_STEPS + 2

            def norm(step, src, dst, stats):
                normalize(nc, step, src, dst, EPS_LN, stats)

            def first(g, par):
                step = Steps(dve, s_d1, g * D1, spare[:])
                dve.wait_ge(s_x[par], (g + 2 - par) * 8 + ONE)
                wait(dve, s_pool, (g - 1) * POOL_N)
                wait(dve, s_tx, (g - 1) * KC)
                norm(step, xs[:, par], xn[:, par], stats1)
                nc.vector.memset(spare[:], 0.0).then_inc(s_xn, 1)
                norm(step, xn[:, par], n1r, stats1)
                wait(dve, s_tn, (g - 1) * KC)
                step.did(nc.vector.tensor_tensor(n1r[:], n1r[:], over_tiles(V["g1"], ST), ALU.mult))
                step.settle()
                step.did(nc.vector.tensor_tensor(n1[:, par], n1r[:], over_tiles(V["be1"], ST), ALU.add))
                step.settle()
                nc.vector.memset(spare[:], 0.0).then_inc(s_n1, 1)
                wait(dve, s_va_st, 16 * g)
                dve.wait_ge(s_pool, g * POOL_N + 2 + ONE)
                for i in range(ST):
                    dve.wait_ge(s_vmp, g * ST + i + 1 + ONE)
                    pv = bank[6 + i % 2]
                    nc.vector.tensor_tensor(va[:, i], pv[:, 0:E], V["bv"], ALU.add).then_inc(s_vu, 1)
                    nc.vector.tensor_tensor(n1[:, par, i], n1[:, par, i], pv[:, E:2 * E], ALU.add).then_inc(s_mu, 1)

            D2 = 2 + NORM_STEPS + 2
            D3 = 7 + 2 * ST

            def second(g, par):
                step = Steps(dve, s_d2, g * D2, spare[:])
                dve.wait_ge(s_mu, (g + 1) * ST + ONE)
                dve.wait_ge(s_pool, g * POOL_N + 2 + ONE)
                x1 = acc[:, bass.ds(g * ST, ST)]
                wait(dve, s_t2, g * KC)
                step.did(nc.vector.tensor_tensor(n2[:], n1[:, par], xm[:, par], ALU.add))
                step.settle()
                step.did(nc.vector.tensor_copy(x1, n2[:]))
                norm(step, n2, n1[:, par], stats2)
                step.did(nc.vector.tensor_tensor(n1[:, par], n1[:, par], over_tiles(V["g2"], ST), ALU.mult))
                step.settle()
                step.did(nc.vector.tensor_tensor(n2[:], n1[:, par], over_tiles(V["be2"], ST), ALU.add))
                step.settle()
                nc.vector.memset(spare[:], 0.0).then_inc(s_n2, 1)
                r = Steps(dve, s_d3, g * D3, spare[:])
                dve.wait_ge(s_lg, g + 1 + ONE)
                lg = bank[2][:, 0:ST * NE].rearrange("p (t e) -> p t e", t=ST)
                r.did(nc.vector.tensor_reduce(m8[:], lg, AX.X, ALU.max))
                r.settle()
                nc.vector.tensor_tensor(pr[:], lg, m8[:].to_broadcast([P, ST, NE]), ALU.subtract).then_inc(s_sh, 1)
                dve.wait_ge(s_ex, g + 1 + ONE)
                r.did(nc.vector.tensor_reduce(m8[:], pr[:], AX.X, ALU.add))
                r.settle()
                r.did(nc.vector.reciprocal(m8[:], m8[:]))
                r.settle()
                r.did(nc.vector.tensor_tensor(pr[:], pr[:], m8[:].to_broadcast([P, ST, NE]), ALU.mult))
                r.settle_apart()
                for i in range(ST):
                    r.did(nc.vector.max(top[:, i], pr[:, i]))
                r.settle()
                r.did(nc.vector.memset(top[:, :, TOPK:8], -1.0))
                r.settle_apart()
                for i in range(ST):
                    r.did(nc.vector.match_replace(rest[:, i], top[:, i], pr[:, i], 0.0))
                r.settle()
                r.did(nc.vector.tensor_tensor(cb[:], pr[:], rest[:], ALU.subtract))
                r.settle()
                r.did(nc.vector.tensor_copy(comb[:, bass.ds(g * ST, ST)], cb[:]))
                r.settle()
                nc.vector.memset(spare[:], 0.0).then_inc(s_cb, 1)
                dve.wait_ge(s_b2p, g + 1 + ONE)
                for i in range(2):
                    a2 = acc[:, bass.ds(g * ST + i * 2, 2)]
                    nc.vector.tensor_tensor(a2, a2, bank[4 + i][:].rearrange("p (t e) -> p t e", t=2),
                                            ALU.add).then_inc(s_b2u, 1)

            paired(dve, B, first, second)
            dve.wait_ge(s_b2u, 2 * B + ONE)

        @block.tensor
        def _(pe):
            pe.wait_ge(s_const, 16 * NCONST + ONE)

            def turn(dst, src, done):
                for k in range(KC):
                    for i in range(ST):
                        last = nc.tensor.transpose(dst[k][:, i * P:(i + 1) * P], src[:, i, k * P:(k + 1) * P], ident[:])
                    last.then_inc(done, 1)

            def first(g, par):
                pe.wait_ge(s_xn, g + 1 + ONE)
                turn(bank[0:2], xn[:, par], s_tx)
                pe.wait_ge(s_cx, KC * (g + 1) + ONE)
                wait(pe, s_b2u, 2 * (g - 1))
                for c in range(4):
                    if c >= 2:
                        pe.wait_ge(s_qk, g * 4 + c - 1 + ONE)
                    w = (wq, wk)[c // 2]
                    for k in range(KC):
                        last = nc.tensor.matmul(bank[4 + c % 2][:], w[:, k, (c % 2) * P:(c % 2 + 1) * P],
                                                xnT[:, par, k], start=(k == 0), stop=(k == KC - 1))
                    last.then_inc(s_qkp, 1)
                pe.wait_ge(s_n1, g + 1 + ONE)
                turn(bank[2:4], n1[:, par], s_tn)
                pe.wait_ge(s_cn, KC * (g + 1) + ONE)
                for i in range(ST):
                    wait(pe, s_mu, g * ST + i - 1)
                    for k in range(KC):
                        nc.tensor.matmul(bank[6 + i % 2][:, 0:E], xnT[:, par, k, i * P:(i + 1) * P], wv[:, k],
                                         start=(k == 0), stop=(k == KC - 1))
                    for k in range(KC):
                        last = nc.tensor.matmul(bank[6 + i % 2][:, E:2 * E], n1T[:, par, k, i * P:(i + 1) * P],
                                                mix[:, k], start=(k == 0), stop=(k == KC - 1))
                    last.then_inc(s_vmp, 1)

            def second(g, par):
                pe.wait_ge(s_n2, g + 1 + ONE)
                turn(bank[0:2], n2, s_t2)
                pe.wait_ge(s_c2, KC * (g + 1) + ONE)
                for i in range(ST):
                    for k in range(KC):
                        last = nc.tensor.matmul(bank[2][:, i * NE:(i + 1) * NE], n2T[:, k, i * P:(i + 1) * P],
                                                rw[:, k], start=(k == 0), stop=(k == KC - 1))
                last.then_inc(s_lg, 1)
                pe.wait_ge(s_cb, g + 1 + ONE)
                for i in range(ST):
                    last = nc.tensor.transpose(bank[3][0:NE, i * P:(i + 1) * P], cb[:, i], ident[:])
                last.then_inc(s_ct, 1)
                pe.wait_ge(s_cc, g + 1 + ONE)
                if isinstance(g, int) and g == B - 1:
                    pe.wait_ge(s_qk, 4 * B + ONE)
                else:
                    pe.wait_ge(s_qk, (g + 2) * 4 + ONE)
                for i in range(ST):
                    last = nc.tensor.matmul(bank[4 + i // 2][:, (i % 2) * E:(i % 2 + 1) * E], cT[:, i * P:(i + 1) * P],
                                            b2[:], start=True, stop=True)
                last.then_inc(s_b2p, 1)

            paired(pe, B, first, second)


def experts(nc, t, keep):
    with ExitStack() as ctx:
        def sb(name, shape, dt=F32):
            return ctx.enter_context(nc.sbuf_tensor(name, shape, dt))

        sems = []

        def sem(name):
            sems.append(ctx.enter_context(nc.semaphore(name)))
            return sems[-1]

        def dma_sem(name):
            return ctx.enter_context(nc.semaphore(name))

        acc, comb, tabq, tabk = keep["acc"], keep["comb"], keep["tabq"], keep["tabk"]
        up = [ctx.enter_context(nc.psum_tensor(f"up{i}", [P, 512], F32)) for i in range(2)]
        dn = [ctx.enter_context(nc.psum_tensor(f"dn{i}", [P, 512], F32)) for i in range(2)]
        rl = [ctx.enter_context(nc.psum_tensor(f"rl{i}", [P, 2, 512], F32)) for i in range(2)]
        w1 = [[sb(f"w1_{a}{i}", [P, KC, F]) for i in range(2)] for a in "hl"]
        w2 = [[sb(f"w2_{a}{i}", [P, FC, E]) for i in range(2)] for a in "hl"]
        b1 = sb("b1_sb", [P, NE, FC])
        tok = [[sb(f"tok_{a}{i}", [P, KC, S]) for i in range(2)] for a in "hl"]
        hid = [sb(f"hid_{a}", [P, FC, S]) for a in "hl"]
        raw = sb("hid_raw", [P, 2, S])
        PRODUCTS = [(0, 0), (0, 1), (1, 0)]
        stack = [sb(f"stack{i}", [KS, BH, LB], BF16) for i in range(2)]
        rel = sb("rel", [P, 2, 4, S])

        s_b1 = dma_sem("b1_loaded")
        s_w = [sem(f"w_loaded{i}") for i in range(2)]
        s_st = [sem(f"stack_loaded{i}") for i in range(2)]
        s_tok = [sem(f"tok_loaded{i}") for i in range(2)]
        s_hh, s_lo = sem("hid_high"), sem("hid_low")
        s_up, s_h, s_dn, s_y = sem("up_done"), sem("hid_ready"), sem("down_done"), sem("y_added")
        s_rm, s_ra, s_rv = sem("rel_done"), sem("rel_by_act"), sem("rel_by_dve")
        s_rs = [sem(f"rel_stored{i}") for i in range(2)]
        GH = B // 2

        start_at_one(nc, sems)
        block = ctx.enter_context(nc.Block())

        def steps(eng, body):
            with eng.Fori(0, NE // 2) as e2:
                for par in range(2):
                    for half in range(2):
                        with eng.Fori(0, GH) as gi:
                            body(e2 * 2 + par, e2, par, half, gi)

        def number(e, half, gi):
            return e * (2 * GH) + half * GH + gi

        @block.sync
        def _(sp):
            def load_tokens(g, slot):
                for a in range(2):
                    sp.dma_start(tok[a][slot][:].rearrange("p k s -> p (k s)"), t["toks"][a, g * P:(g + 1) * P]).then_inc(s_tok[slot], 16)

            for slot in range(2):
                load_tokens(slot, slot)
            with sp.Fori(0, NE) as e:
                for g in range(2 * GH):
                    half, gi = g // GH, g % GH
                    n = e * (2 * GH) + g
                    dst = (t["relq"], t["relk"])[half]
                    for j in range(4):
                        sp.wait_ge(s_ra, n * 4 + j + 1 + ONE)
                        sp.wait_ge(s_rv, n * 4 + j + 1 + ONE)
                        at = (e * LB + (gi * RU + j * 4)) * S
                        sp.dma_start(dst[:, bass.ds(at, 4 * S)], rel[:, j % 2].rearrange("p u s -> p (u s)")).then_inc(s_rs[j % 2], 16)
                    sp.wait_ge(s_up, (n + 1) * FC + ONE)
                    load_tokens((g + 2) % (2 * GH), g % 2)
            for j in range(2):
                sp.wait_ge(s_rs[j], 32 * NE * 2 * GH + ONE)
                sp.wait_ge(s_tok[j], 32 * (NE * GH + 1) + ONE)

        @block.gpsimd
        def _(pool):
            pool.dma_start(b1[:], t["b1"]).then_inc(s_b1, 16)

        @block.scalar
        def _(act):
            def load_weights(e, par):
                wait(act, s_dn, (e - 1) * (2 * GH * ST))
                for a in range(2):
                    act.dma_start(w1[a][par][:].rearrange("p k f -> p (k f)"), t["w1s"][a, bass.ds(e * P, P)]).then_inc(s_w[par], 16)
                    act.dma_start(w2[a][par][:].rearrange("p k f -> p (k f)"), t["w2s"][a, bass.ds(e * P, P)]).then_inc(s_w[par], 16)

            def load_stack(e, half):
                wait(act, s_rm, (e * 2 - 1 + half) * (GH * FC))
                for i, pair in enumerate(PAIRS):
                    src = (t["qparts"], t["kparts"])[half][pair[0]]
                    src = src.rearrange("b (h d) s -> d (b h) s", d=D)[:, :, bass.ds(e * LB, LB)]
                    act.dma_start(stack[half][i * D:(i + 1) * D], src).then_inc(s_st[half], 16)

            def turn(e, par, last=False):
                load_stack(e, 1)
                with act.Fori(0, GH) as gi:
                    body(e, None, par, 0, gi)
                if not last:
                    load_weights(e + 1, 1 - par)
                    load_stack(e + 1, 0)
                with act.Fori(0, GH) as gi:
                    body(e, None, par, 1, gi)

            def body(e, e2, par, half, gi):
                n = number(e, half, gi)
                for j in range(4):
                    for f in range(4 * j, 4 * j + 4) if j < 2 else ():
                        act.wait_ge(s_up, n * FC + f + 1 + ONE)
                        act.wait_ge(s_lo, n * FC + max(f - 1, 0) + ONE)
                        nc.scalar.activation(raw[:, f % 2], up[f % 2][:], ACT.Silu,
                                             bias=b1[:, bass.ds(e, 1), f:f + 1].rearrange("p a b -> p (a b)")).then_inc(s_h, 1)
                        act.wait_ge(s_h, n * FC + f + 1 + ONE)
                        nc.scalar.copy(hid[0][:, f].bitcast(FR), raw[:, f % 2]).then_inc(s_hh, 1)
                    act.wait_ge(s_rm, n * FC + 2 * j + 1 + ONE)
                    act.wait_ge(s_rs[j % 2], n * 32 + 16 * (j // 2) + ONE)
                    nc.scalar.copy(rel[:, j % 2, 0:2], rl[0][:]).then_inc(s_ra, 1)

            load_weights(0, 0)
            load_stack(0, 0)
            act.wait_ge(s_b1, 16)
            with act.Fori(0, NE // 2 - 1) as e2:
                for par in range(2):
                    turn(e2 * 2 + par, par)
            turn(NE - 2, 0)
            turn(NE - 1, 1, last=True)

        @block.vector
        def _(dve):
            def add_outputs(e, n, g, tiles):
                for i in tiles:
                    dve.wait_ge(s_dn, n * ST + i + 1 + ONE)
                    a1 = acc[:, bass.ds(g * ST + i, 1)].rearrange("p o e -> p (o e)")
                    c1 = comb[:, bass.ds(g * ST + i, 1), bass.ds(e, 1)].rearrange("p a b -> p (a b)")
                    nc.vector.scalar_tensor_tensor(a1, dn[i % 2][:, 0:E], c1, a1, ALU.mult, ALU.add).then_inc(s_y, 1)

            def body(e, e2, par, half, gi):
                n = number(e, half, gi)
                g = gi + half * GH
                wait(dve, s_y, n * ST)
                for j in range(4):
                    for f in range(4 * j, 4 * j + 4) if j < 2 else ():
                        dve.wait_ge(s_hh, n * FC + f + 1 + ONE)
                        nc.vector.tensor_tensor(hid[1][:, f].bitcast(FR), raw[:, f % 2], hid[0][:, f], ALU.subtract).then_inc(s_lo, 1)
                    if j >= 2:
                        add_outputs(e, n, g, (2 * j - 4, 2 * j - 3))
                    dve.wait_ge(s_rm, n * 8 + 2 * j + 2 + ONE)
                    dve.wait_ge(s_rs[j % 2], n * 32 + 16 * (j // 2) + ONE)
                    nc.vector.tensor_copy(rel[:, j % 2, 2:4], rl[1][:]).then_inc(s_rv, 1)
            steps(dve, body)
            dve.wait_ge(s_y, NE * NT + ONE)

        @block.tensor
        def _(pe):
            def body(e, e2, par, half, gp, slot):
                gi = gp * 2 + slot
                n = number(e, half, gi)
                tab = (tabq, tabk)[half]

                def relative(j):
                    for c in range(2):
                        wait(pe, (s_ra, s_rv)[c], n * 4 + j)
                        for u in range(2):
                            at = j * 4 + c * 2 + u
                            lhs = stack[half][:, :, bass.ds(gi * RU + at, 1)].rearrange("p h o -> p (h o)")
                            rhs = tab[:, bass.ds(first - at, S)]
                            last = nc.tensor.matmul(rl[c][:, u], lhs, rhs, start=True, stop=True)
                        last.then_inc(s_rm, 1)

                first = pe.snap((S - 1) - e * LB - gi * RU)
                pe.wait_ge(s_w[par], e2 * 64 + 64 + ONE)
                pe.wait_ge(s_tok[slot], (e * GH + (half * (GH // 2) + 1) + gp) * 32 + ONE)
                pe.wait_ge(s_st[half], (e + 1) * 16 * len(PAIRS) + ONE)
                for f in range(FC):
                    if f >= 2:
                        pe.wait_ge(s_h, n * FC + f - 1 + ONE)
                    for k in range(KC):
                        for m, (a, c) in enumerate(PRODUCTS):
                            last = nc.tensor.matmul(up[f % 2][:], w1[a][par][:, k, f * P:(f + 1) * P].bitcast(FR),
                                                    tok[c][slot][:, k].bitcast(FR), start=(k == 0 and m == 0),
                                                    stop=(k == KC - 1 and m == len(PRODUCTS) - 1))
                    last.then_inc(s_up, 1)
                    if f % 4 == 3:
                        relative(f // 4)
                for i in range(ST):
                    wait(pe, s_y, n * ST + max(i - 1, 0))
                    for f in range(FC):
                        if i == 0:
                            pe.wait_ge(s_lo, n * FC + f + 1 + ONE)
                        for m, (a, c) in enumerate(PRODUCTS):
                            last = nc.tensor.matmul(dn[i % 2][:, 0:E], hid[a][:, f, i * P:(i + 1) * P].bitcast(FR),
                                                    w2[c][par][:, f].bitcast(FR), start=(f == 0 and m == 0),
                                                    stop=(f == FC - 1 and m == len(PRODUCTS) - 1))
                    last.then_inc(s_dn, 1)
                    if i % 2:
                        relative(2 + i // 2)

            with pe.Fori(0, NE // 2) as e2:
                for par in range(2):
                    for half in range(2):
                        with pe.Fori(0, GH // 2) as gp:
                            for slot in range(2):
                                body(e2 * 2 + par, e2, par, half, gp, slot)


def attention(nc, t, keep):
    with ExitStack() as ctx:
        def sb(name, shape, dt=F32):
            return ctx.enter_context(nc.sbuf_tensor(name, shape, dt))

        sems = []

        def sem(name):
            sems.append(ctx.enter_context(nc.semaphore(name)))
            return sems[-1]

        def dma_sem(name):
            return ctx.enter_context(nc.semaphore(name))

        ident, acc = keep["ident"], keep["acc"]
        HG = 4
        RB = HG
        NG = H // HG
        sc = [ctx.enter_context(nc.psum_tensor(f"sc{i}", [P, S], F32)) for i in range(2)]
        pt = [ctx.enter_context(nc.psum_tensor(f"pt{i}", [P, S], F32)) for i in range(2)]
        cx = [ctx.enter_context(nc.psum_tensor(f"cx{i}", [P, S], F32)) for i in range(2)]
        wo_ps = [ctx.enter_context(nc.psum_tensor(f"wo_ps{i}", [P, S], F32)) for i in range(2)]
        wo = sb("wo_sb", [P, NG, E])
        gb = sb("gamma_beta", [P, 2, E])
        rq = [sb(f"rq{i}", [P, ST, S]) for i in range(RB)]
        rk = [sb(f"rk{i}", [P, ST, S]) for i in range(RB)]
        qs = [sb(f"qs{i}", [KS, HG, S], BF16) for i in range(2)]
        ks = [sb(f"ks{i}", [KS, HG, S], BF16) for i in range(2)]
        vs = [sb(f"vs{i}", [P, ST, HG * D]) for i in range(2)]
        sm = sb("scores", [P, 2, ST, S])
        mx = sb("row_max", [P, 2, ST])
        nb = sb("neg_max", [P, 2, ST])
        pT = sb("probsT", [P, HG, ST, S])
        es = sb("exp_sum", [P, 2, ST, HG])
        er = sb("exp_recip", [P, ST * HG])
        ex = sb("recip_spread", [P, 2, ST, HG * 32])
        rc = sb("recip_rows", [P, S])
        cT = sb("ctxT", [P, NG, S])
        xo = sb("xo", [P, ST, E])
        xx = sb("xx", [P, ST, E])
        hh = sb("hh", [P, ST, E])
        oo = sb("oo", [P, ST, E])
        stats = sb("att_stats", [P, ST, 6]), sb("att_mv", [P, ST, 2]), sb("att_work", [P, 3, ST])

        s_const = sem("consts_loaded")
        s_rq = [sem(f"rq_loaded{i}") for i in range(RB)]
        s_rk = [sem(f"rk_loaded{i}") for i in range(RB)]
        s_qkv = [sem(f"qkv_loaded{i}") for i in range(2)]
        s_zero = sem("ctx_zeroed")
        s_sc, s_su = sem("scores_done"), sem("scores_taken")
        s_d = sem("dve_max_steps")
        s_nb, s_e = sem("neg_max_ready"), sem("exp_done")
        s_pt, s_pa, s_pd = sem("probs_turned"), sem("probsT_by_act"), sem("probsT_by_dve")
        s_pv, s_er, s_bc, s_n = sem("ctx_done"), sem("recips_ready"), sem("recips_spread"), sem("norm_steps")
        s_inv = sem("sums_inverted")
        s_wo, s_h, s_f = sem("wo_done"), sem("out_norm_steps"), sem("final_steps")
        s_xl, s_g, s_out = dma_sem("x_reloaded"), sem("gate_ready"), dma_sem("out_stored")
        RQ0 = (RB - 1) * ST
        PV0 = 1
        F_STEPS = 6
        NQKV = 2 * len(PAIRS) + 1
        spare = sb("att_spare", [P, ST + 1])
        pad = sb("pool_spare", [P, 2])
        s_pad = sem("pool_spare_set")

        start_at_one(nc, sems, [(s_sc, RQ0), (s_su, RQ0), (s_pv, PV0)])
        block = ctx.enter_context(nc.Block())

        @block.sync
        def _(sp):
            sp.dma_start(wo[:], t["wo"]).then_inc(s_const, 16)
            sp.dma_start(gb[:], t["vecs"][VECS.index("ln_gamma"):VECS.index("ln_beta") + 1].partition_broadcast(P)).then_inc(s_const, 16)
            with sp.Fori(0, B) as b:
                for hg in range(NG):
                    i = hg % 2
                    sp.wait_ge(s_pv, b * NG + (hg - 1 + PV0) + ONE)
                    for dst, name, side in ((qs, "qparts", 0), (ks, "kparts", 1)):
                        for n, pair in enumerate(PAIRS):
                            src = t[name][pair[side], bass.ds(b, 1)].rearrange("o (h d) s -> d (o h) s", d=D)
                            sp.dma_start(dst[i][n * D:(n + 1) * D], src[:, hg * HG:(hg + 1) * HG]).then_inc(s_qkv[i], 16)
                    src = t["va"][bass.ds(b * S, S)].rearrange("(t p) e -> p t e", p=P)
                    sp.dma_start(vs[i][:], src[:, :, hg * HG * D:(hg + 1) * HG * D]).then_inc(s_qkv[i], 16)
                    for j in range(HG):
                        n = b * H + (hg * HG + j)
                        sp.wait_ge(s_sc, n * ST + ONE)
                        sp.wait_ge(s_su, n * ST + ONE)
                        for dst, name, done in ((rk, "relk", s_rk), (rq, "relq", s_rq)):
                            src = t[name][bass.ds(n, 1), 0:S * S].rearrange("o (t p s) -> p (o t) s", p=P, s=S)
                            sp.dma_start(dst[j][:], src).then_inc(done[j], 16)

        @block.gpsimd
        def _(pool):
            nc.gpsimd.memset(pad[:, 0:1], 0.0).then_inc(s_pad, 1)
            pool.wait_ge(s_pad, 1 + ONE)
            pool.wait_ge(s_const, 32 + ONE)
            with pool.Fori(0, B) as b:
                pool.wait_ge(s_f, b * F_STEPS + ONE)
                pool.dma_start(xo[:], t["xnbo"][bass.ds(b * S, S)].rearrange("(t p) e -> p t e", p=P)).then_inc(s_xl, 16)
                pool.dma_start(xx[:], t["x"][bass.ds(b * S, S)].rearrange("(t p) e -> p t e", p=P)).then_inc(s_xl, 16)
                step = Steps(pool, s_f, b * F_STEPS)
                pool.wait_ge(s_h, (b + 1) * (2 + NORM_STEPS) + ONE)
                step.did(nc.gpsimd.tensor_tensor(oo[:], oo[:], over_tiles(gb[:, 0], ST), ALU.mult))
                step.settle()
                step.did(nc.gpsimd.tensor_tensor(oo[:], oo[:], over_tiles(gb[:, 1], ST), ALU.add))
                step.settle()
                pool.wait_ge(s_g, b + 1 + ONE)
                step.did(nc.gpsimd.tensor_tensor(oo[:], oo[:], acc[:, bass.ds(b * ST, ST)], ALU.mult))
                step.settle()
                step.did(nc.gpsimd.tensor_tensor(oo[:], oo[:], xx[:], ALU.add))
                step.settle()
                step.did(nc.gpsimd.tensor_tensor(pad[:, 1:2], pad[:, 0:1], pad[:, 0:1], ALU.add))
                pool.dma_start(t["out"][bass.ds(b * S, S)].rearrange("(t p) e -> p t e", p=P), oo[:]).then_inc(s_out, 16)
                step.settle()
                pool.wait_ge(s_out, (b + 1) * 16)
                step.did(nc.gpsimd.tensor_tensor(pad[:, 1:2], pad[:, 0:1], pad[:, 0:1], ALU.add))
            pool.wait_ge(s_out, 16 * B)


        def rounds(eng, score, rest, finish_group, finish_batch):
            score(0, 0, 0, 0)

            def batch(b, last):
                for h in range(H):
                    hg, j = h // HG, h % HG
                    if h < H - 1:
                        score(b, h + 1, (h + 1) // HG, (h + 1) % HG)
                    elif not last:
                        score(b + 1, 0, 0, 0)
                    rest(b, h, hg, j)
                    if h > 0 and j == 0:
                        finish_group(b, hg - 1)
                    if h == 0 and not (isinstance(b, int) and b == 0):
                        finish_group(b - 1, NG - 1)
                    if h == 1 and not (isinstance(b, int) and b == 0):
                        finish_batch(b - 1)

            batch(0, False)
            with eng.Fori(1, B - 1) as b:
                batch(b, False)
            batch(B - 1, True)
            finish_group(B - 1, NG - 1)
            finish_batch(B - 1)

        @block.scalar
        def _(act):
            def score(b, h, hg, j):
                head = b * H + h
                if j == 0 and not (isinstance(b, int) and b == 0 and hg < 2):
                    act.wait_ge(s_er, b * NG + (hg - 1) + ONE)
                for i in range(ST):
                    act.wait_ge(s_nb, head + 1 + ONE)
                    nc.scalar.activation(sm[:, j % 2, i], sm[:, j % 2, i], ACT.Exp, bias=nb[:, j % 2, i:i + 1],
                                         scale=SM_SCALE, accum_out=es[:, hg % 2, i, j:j + 1]).then_inc(s_e, 1)

            def rest(b, h, hg, j):
                head = b * H + h
                for i in range(0, ST, 2):
                    act.wait_ge(s_pt, head * ST + i + 1 + ONE)
                    nc.scalar.copy(pT[:, j, i], pt[0][:]).then_inc(s_pa, 1)

            def gate(b):
                nc.scalar.activation(acc[:, bass.ds(b * ST, ST)], acc[:, bass.ds(b * ST, ST)], ACT.Silu).then_inc(s_g, 1)

            def batch(b, last):
                for h in range(H):
                    rest(b, h, h // HG, h % HG)
                    if h < H - 1:
                        score(b, h + 1, (h + 1) // HG, (h + 1) % HG)
                    elif not last:
                        score(b + 1, 0, 0, 0)
                gate(b)

            score(0, 0, 0, 0)
            batch(0, False)
            with act.Fori(1, B - 1) as b:
                batch(b, False)
            batch(B - 1, True)

        @block.vector
        def _(dve):
            for i in range(2):
                nc.vector.memset(cx[i][:], 0.0).then_inc(s_zero, 1)

            def score(b, h, hg, j):
                head = b * H + h
                step = Steps(dve, s_d, head * ST)
                dve.wait_ge(s_rq[j], (b * NG + (hg + 1)) * 16 + ONE)
                wait(dve, s_pt, (head - 1) * ST)
                for i in range(ST):
                    dve.wait_ge(s_sc, head * ST + (i + 1 + RQ0) + ONE)
                    nc.vector.memset(spare[:, i:i + 1], 0.0)
                    nc.vector.tensor_tensor_reduce(sm[:, j % 2, i], sc[i % 2][:], rq[j][:, i], 1.0, -3.0e38,
                                                   ALU.add, ALU.max, mx[:, j % 2, i:i + 1]).then_inc(s_su, 1)
                dve.wait_ge(s_su, head * ST + (ST + RQ0) + ONE)
                nc.vector.tensor_scalar(nb[:, j % 2], mx[:, j % 2], -SM_SCALE, None, ALU.mult).then_inc(s_nb, 1)

            def rest(b, h, hg, j):
                head = b * H + h
                for i in range(1, ST, 2):
                    dve.wait_ge(s_pt, head * ST + i + 1 + ONE)
                    nc.vector.tensor_copy(pT[:, j, i], pt[1][:]).then_inc(s_pd, 1)
                if j == HG - 1:
                    if not (isinstance(b, int) and b == 0 and hg < 2):
                        dve.wait_ge(s_bc, b * NG + (hg - 1) + ONE)
                    dve.wait_ge(s_e, (head + 1) * ST + ONE)
                    nc.vector.reciprocal(er[:], es[:, hg % 2].rearrange("p t h -> p (t h)")).then_inc(s_inv, 1)
                    dve.wait_ge(s_inv, b * NG + (hg + 1) + ONE)
                    nc.vector.tensor_copy(ex[:, hg % 2].rearrange("p t (h k) -> p (t h) k", k=32),
                                          er[:].unsqueeze(2).to_broadcast([P, ST * HG, 32])).then_inc(s_er, 1)

            def finish_group(b, hg):
                group = b * NG + hg
                step = Steps(dve, s_n, group * 2)
                dve.wait_ge(s_bc, group + 1 + ONE)
                step.did(nc.vector.tensor_copy(rc[:], wo_ps[0][:]))
                step.settle()
                dve.wait_ge(s_pv, group + (1 + PV0) + ONE)
                dve.wait_ge(s_wo, b * 2 + ONE)
                step.did(nc.vector.tensor_tensor(cT[:, hg], cx[hg % 2][:], rc[:], ALU.mult))

            def finish_batch(b):
                step = Steps(dve, s_h, b * (2 + NORM_STEPS), spare[:, ST:ST + 1])
                dve.wait_ge(s_xl, (b + 1) * 32)
                for i in range(2):
                    dve.wait_ge(s_wo, b * 2 + i + 1 + ONE)
                    step.did(nc.vector.tensor_tensor(hh[:, 2 * i:2 * i + 2], wo_ps[i][:].rearrange("p (t e) -> p t e", t=2),
                                                     xo[:, 2 * i:2 * i + 2], ALU.add))
                step.settle()
                dve.wait_ge(s_f, b * F_STEPS + ONE)
                normalize(nc, step, hh, oo, EPS_ATT, stats)

            rounds(dve, score, rest, finish_group, finish_batch)

        @block.tensor
        def _(pe):
            pe.wait_ge(s_const, 32 + ONE)
            pe.wait_ge(s_zero, 2 + ONE)

            def score(b, h, hg, j):
                head = b * H + h
                g2 = hg % 2
                pe.wait_ge(s_rk[j], (b * NG + (hg + 1)) * 16 + ONE)
                if j == 0:
                    pe.wait_ge(s_qkv[g2], (b * 2 + (hg // 2 + 1)) * (16 * NQKV) + ONE)
                for i in range(ST):
                    if not (isinstance(head, int) and head == 0 and i < 2):
                        pe.wait_ge(s_su, head * ST + (i - 1 + RQ0) + ONE)
                    for r in range(ST):
                        nc.tensor.matmul(sc[i % 2][:, r * P:(r + 1) * P], rk[j][:, r, i * P:(i + 1) * P], ident[:],
                                         start=(r == 0), stop=False, is_transpose=True, skip_group_check=True)
                    nc.tensor.matmul(sc[i % 2][:], qs[g2][:, j, i * P:(i + 1) * P], ks[g2][:, j], start=False,
                                     stop=True, skip_group_check=True).then_inc(s_sc, 1)

            def rest(b, h, hg, j):
                head = b * H + h
                pe.wait_ge(s_e, (head + 1) * ST + ONE)
                for r in range(ST):
                    who, at = (s_pa, s_pd)[r % 2], head * (ST // 2) + r // 2
                    wait(pe, who, at)
                    for i in range(ST):
                        last = nc.tensor.transpose(pt[r % 2][:, i * P:(i + 1) * P], sm[:, j % 2, i, r * P:(r + 1) * P], ident[:])
                    last.then_inc(s_pt, 1)
                if j == HG - 1:
                    group = b * NG + hg
                    pe.wait_ge(s_pa, (head + 1) * (ST // 2) + ONE)
                    pe.wait_ge(s_pd, (head + 1) * (ST // 2) + ONE)
                    if not (isinstance(b, int) and b == 0 and hg < 2):
                        pe.wait_ge(s_n, (group - 1) * 2 + ONE)
                    for r in range(ST):
                        for k in range(HG):
                            last = nc.tensor.matmul(cx[hg % 2][32 * k:32 * k + D], vs[hg % 2][:, r, k * D:(k + 1) * D],
                                                    pT[:, k, r], start=(r == 0), stop=(r == ST - 1), skip_group_check=True)
                    last.then_inc(s_pv, 1)

            def finish_group(b, hg):
                group = b * NG + hg
                pe.wait_ge(s_er, group + 1 + ONE)
                if not (isinstance(b, int) and b == 0 and hg == 0):
                    pe.wait_ge(s_n, group * 2 + ONE)
                if hg == 0:
                    pe.wait_ge(s_h, b * (2 + NORM_STEPS) + ONE)
                for i in range(ST):
                    last = nc.tensor.matmul(wo_ps[0][:, i * P:(i + 1) * P],
                                            ex[:, hg % 2, i], ident[:],
                                            start=True, stop=True, skip_group_check=True)
                last.then_inc(s_bc, 1)

            def finish_batch(b):
                pe.wait_ge(s_n, (b + 1) * (NG * 2) + ONE)
                for i in range(ST):
                    for k in range(NG):
                        last = nc.tensor.matmul(wo_ps[i // 2][:, (i % 2) * E:(i % 2 + 1) * E], cT[:, k, i * P:(i + 1) * P],
                                                wo[:, k], start=(k == 0), stop=(k == NG - 1), skip_group_check=True)
                    if i % 2:
                        last.then_inc(s_wo, 1)

            rounds(pe, score, rest, finish_group, finish_batch)


def program(nc, t):
    with ExitStack() as ctx:
        def sb(name, shape, dt=F32):
            return ctx.enter_context(nc.sbuf_tensor(name, shape, dt))

        keep = {
            "ident": sb("ident", [P, P]),
            "acc": sb("acc", [P, NT, E]),
            "comb": sb("comb", [P, NT, NE]),
            "tabq": sb("tabq", [KS, WIN], BF16),
            "tabk": sb("tabk", [KS, WIN], BF16),
        }
        prep(nc, t, keep)
        experts(nc, t, keep)
        attention(nc, t, keep)


def kernel(**inputs):
    import numpy as np
    import concourse.bacc as bacc
    from concourse.bass_utils import run_bass_kernel_spmd

    a = {n: np.ascontiguousarray(v) for n, v in inputs.items()}
    x = a["L0_attn_hidden_states"]
    emb = a["L0_attn_dist_emb"]
    dist = S - 1 - np.arange(WIN)
    row = dist + M_POS - 1
    row = np.where(row < 0, row + emb.shape[0], row)
    row = np.clip(row, 0, emb.shape[0] - 1)
    tabq = emb[row].T
    tabk = np.concatenate([tabq[:, WIN - 2::-1], tabq[:, :1]], axis=1)
    wo = np.zeros((H // 4, 4, 32, E), np.float32)
    wo[:, :, :D] = a["L0_attn_Wo"].reshape(H // 4, 4, D, E)
    mask = np.array([[-(p[1] > 0), -(p[1] > 1)] for p in PAIRS], np.float32).repeat(D, axis=0)
    f = {"bv": "L0_attn_bv", "bo": "L0_attn_bo", "mix_b": "L0_ffn_mix_b", "g1": "L0_ffn_g1", "be1": "L0_ffn_be1",
         "g2": "L0_ffn_g2", "be2": "L0_ffn_be2", "ln_gamma": "L0_attn_ln_gamma", "ln_beta": "L0_attn_ln_beta"}
    arrays = {
        "x": x.reshape(B * S, E),
        "Wq": a["L0_attn_Wq"], "Wk": a["L0_attn_Wk"], "Wv": a["L0_attn_Wv"],
        "mix_w": a["L0_ffn_mix_w"], "router_w": a["L0_ffn_router_w"],
        "wo": wo.reshape(H // 4, P, E).transpose(1, 0, 2),
        "w1": a["L0_ffn_w1"], "w2": a["L0_ffn_w2"],
        "b1": a["L0_ffn_b1"].reshape(NE, FC, P).transpose(2, 0, 1),
        "b2": a["L0_ffn_b2"],
        "bqk": np.stack([a["L0_attn_bq"], a["L0_attn_bk"]]).reshape(2 * KC, P).T,
        "vecs": np.stack([a[f[n]] for n in VECS]),
        "tabq": np.tile(tabq, (len(PAIRS), 1)), "tabk": np.tile(tabk, (len(PAIRS), 1)),
        "mask": mask, "ident": np.eye(P, dtype=np.float32),
    }
    nc = bacc.Bacc("TRN2", target_bir_lowering=False, num_devices=1)
    t, ins = {}, {}
    for name, v in arrays.items():
        v = np.ascontiguousarray(v)
        ins[f"in_{name}"] = v
        t[name] = nc.dram_tensor(f"in_{name}", v.shape, mybir.dt.from_np(v.dtype), kind="ExternalInput").ap()
    for name, shape, dt in (("qparts", (PARTS, B, E, S), BF16), ("kparts", (PARTS, B, E, S), BF16),
                            ("xnbo", (B * S, E), F32), ("va", (B * S, E), F32), 
                            ("w1s", (2, NE * P, KC * F), F32), ("w2s", (2, NE * P, FC * E), F32),
                            ("toks", (2, B * P, KC * S), F32),
                            ("relq", (BH, PITCH), F32), ("relk", (BH, PITCH), F32)):
        t[name] = nc.dram_tensor(f"scratch_{name}", shape, dt).ap()
    t["out"] = nc.dram_tensor("out_0", (B * S, E), F32, kind="ExternalOutput").ap()
    program(nc, t)
    got = run_bass_kernel_spmd(nc, [ins], core_ids=[0])
    return got.results[0]["out_0"].reshape(B, S, E)
```
